# Optimizing a Trainium2 kernel written in Bass

```python
import numpy as np
import jax
import jax.numpy as jnp

def _softmax(x, axis=-1):
    return jax.nn.softmax(x, axis=axis)
def _gelu(x):
    return jax.nn.gelu(x, approximate=True)
def _silu(x):
    return jax.nn.silu(x)
def _sigmoid(x):
    return jax.nn.sigmoid(x)
def _layernorm(x, axis=-1, eps=1e-5):
    m = jnp.mean(x, axis=axis, keepdims=True)
    v = jnp.var(x, axis=axis, keepdims=True)
    return (x - m) / jnp.sqrt(v + eps)
def _scatter_add(tgt, idx, src, axis=0):
    return tgt.at[idx].add(src)
def _segment_sum(src, seg, n):
    return jax.ops.segment_sum(src, seg, n)

kernel_name = 'mk_conv_preact_d2_conv_nchw512_3983f2'

def setup_inputs(seed: int = 0):
    np.random.seed(seed)
    _w = jnp.asarray
    def _rec_inputs():
        import jax
        import jax.numpy as jnp
        _gk = jax.random.key(seed)
        x = 0.0002103 + 1 * jax.random.normal(jax.random.fold_in(_gk, 1), (16, 512, 64, 64), jnp.float32)
        return x
    x = _rec_inputs()
    def _L0_conv_setup():
        import jax, jax.numpy as jnp
        import numpy as np
        PAD0, PAD1 = (2, 1)

        def make_kernel(k1d):
            k = jnp.asarray(k1d, dtype=jnp.float32)
            k = k[None, :] * k[:, None]
            return k / k.sum()
        key = jax.random.key(seed)
        x = jax.random.normal(key, (16, 512, 64, 64), dtype=jnp.float32)
        kernel = make_kernel([1.0, 3.0, 3.0, 1.0])
        return {'x': x, 'kernel': kernel}
    _L0_conv_all = _L0_conv_setup()
    _L0_conv_in = {k: v for k, v in _L0_conv_all.items() if k in ('kernel', )}
    del _L0_conv_all

    def _L1_conv_setup():
        import jax, jax.numpy as jnp
        import numpy as np
        import math
        PERMS = ((0, 1, 2, 3, 4, 5, 6, 7), (3, 0, 1, 2, 5, 6, 7, 4), (2, 3, 0, 1, 6, 7, 4, 5), (1, 2, 3, 0, 7, 4, 5, 6), (4, 5, 6, 7, 0, 1, 2, 3), (5, 6, 7, 4, 3, 0, 1, 2), (6, 7, 4, 5, 2, 3, 0, 1), (7, 4, 5, 6, 1, 2, 3, 0))

        def d4_1x1(x, w):
            b, C, h, ww = x.shape
            cout, cin, _ = w.shape
            W = jnp.stack([w[..., jnp.array(p)] for p in PERMS], axis=1)
            xr = x.reshape(b, cin, 8, h, ww)
            y = jnp.einsum('ogif,bifhw->boghw', W, xr)
            return y.reshape(b, cout * 8, h, ww)

        def group_norm(x, gamma, beta, num_groups, eps=1e-05):
            b, C, h, w = x.shape
            xg = x.reshape(b, num_groups, C // num_groups, h, w)
            mean = xg.mean(axis=(2, 3, 4), keepdims=True)
            var = xg.var(axis=(2, 3, 4), keepdims=True)
            xn = ((xg - mean) / jnp.sqrt(var + eps)).reshape(b, C, h, w)
            return xn * gamma[None, :, None, None] + beta[None, :, None, None]

        def unfold_patches(x, k):
            b, C, h, w = x.shape
            p = (k - 1) // 2
            xp = jnp.pad(x, ((0, 0), (0, 0), (p, p), (p, p)))
            pats = jnp.stack([xp[:, :, i:i + h, j:j + w] for i in range(k) for j in range(k)], axis=2)
            return pats
        key = jax.random.key(seed)
        ks = jax.random.split(key, 4)
        b, H, W = (8, 56, 56)
        cin, cout, rr, k, gc = (64, 64, 2, 3, 16)
        cmid = cin // rr
        G = cout // gc
        x = jax.random.normal(ks[0], (b, cin * 8, H, W), jnp.float32)
        w_v = jax.random.normal(ks[1], (cout, cin, 8), jnp.float32) / math.sqrt(8 * cin / 2)
        w1 = jax.random.normal(ks[2], (cmid, cin, 8), jnp.float32) / math.sqrt(8 * cin / 2)
        gn_gamma = jnp.ones((cmid * 8,), jnp.float32)
        gn_beta = jnp.zeros((cmid * 8,), jnp.float32)
        w2 = jax.random.normal(ks[3], (k * k * G, cmid), jnp.float32) / math.sqrt(cmid)
        b2 = jnp.zeros((k * k * G,), jnp.float32)
        return {'x': x, 'w_v': w_v, 'w1': w1, 'gn_gamma': gn_gamma, 'gn_beta': gn_beta, 'w2': w2, 'b2': b2}
    _L1_conv_all = _L1_conv_setup()
    _L1_conv_in = {k: v for k, v in _L1_conv_all.items() if k in ('w_v', 'w1', 'gn_gamma', 'gn_beta', 'w2', 'b2', )}
    del _L1_conv_all

    return {
        "x": x,
        "L0_conv_kernel": _L0_conv_in["kernel"],
        "L1_conv_w_v": _L1_conv_in["w_v"],
        "L1_conv_w1": _L1_conv_in["w1"],
        "L1_conv_gn_gamma": _L1_conv_in["gn_gamma"],
        "L1_conv_gn_beta": _L1_conv_in["gn_beta"],
        "L1_conv_w2": _L1_conv_in["w2"],
        "L1_conv_b2": _L1_conv_in["b2"],
    }

def reference(x, L0_conv_kernel, L1_conv_w_v, L1_conv_w1, L1_conv_gn_gamma, L1_conv_gn_beta, L1_conv_w2, L1_conv_b2):
    import jax
    import jax.numpy as jnp
    def _L0_conv_ref(x, kernel):
        import jax, jax.numpy as jnp
        import numpy as np
        PAD0, PAD1 = (2, 1)

        def make_kernel(k1d):
            k = jnp.asarray(k1d, dtype=jnp.float32)
            k = k[None, :] * k[:, None]
            return k / k.sum()
        N, C, H, W = x.shape
        kh, kw = kernel.shape
        w = jnp.flip(kernel, (0, 1))[None, None]
        xr = x.reshape(N * C, 1, H, W)
        out = jax.lax.conv_general_dilated(xr, w, window_strides=(1, 1), padding=((PAD0, PAD1), (PAD0, PAD1)), dimension_numbers=('NCHW', 'OIHW', 'NCHW'))
        Ho = H + PAD0 + PAD1 - kh + 1
        Wo = W + PAD0 + PAD1 - kw + 1
        return out.reshape(N, C, Ho, Wo)

    def _L1_conv_ref(x, w_v, w1, gn_gamma, gn_beta, w2, b2):
        import jax, jax.numpy as jnp
        import numpy as np
        import math
        PERMS = ((0, 1, 2, 3, 4, 5, 6, 7), (3, 0, 1, 2, 5, 6, 7, 4), (2, 3, 0, 1, 6, 7, 4, 5), (1, 2, 3, 0, 7, 4, 5, 6), (4, 5, 6, 7, 0, 1, 2, 3), (5, 6, 7, 4, 3, 0, 1, 2), (6, 7, 4, 5, 2, 3, 0, 1), (7, 4, 5, 6, 1, 2, 3, 0))

        def d4_1x1(x, w):
            b, C, h, ww = x.shape
            cout, cin, _ = w.shape
            W = jnp.stack([w[..., jnp.array(p)] for p in PERMS], axis=1)
            xr = x.reshape(b, cin, 8, h, ww)
            y = jnp.einsum('ogif,bifhw->boghw', W, xr)
            return y.reshape(b, cout * 8, h, ww)

        def group_norm(x, gamma, beta, num_groups, eps=1e-05):
            b, C, h, w = x.shape
            xg = x.reshape(b, num_groups, C // num_groups, h, w)
            mean = xg.mean(axis=(2, 3, 4), keepdims=True)
            var = xg.var(axis=(2, 3, 4), keepdims=True)
            xn = ((xg - mean) / jnp.sqrt(var + eps)).reshape(b, C, h, w)
            return xn * gamma[None, :, None, None] + beta[None, :, None, None]

        def unfold_patches(x, k):
            b, C, h, w = x.shape
            p = (k - 1) // 2
            xp = jnp.pad(x, ((0, 0), (0, 0), (p, p), (p, p)))
            pats = jnp.stack([xp[:, :, i:i + h, j:j + w] for i in range(k) for j in range(k)], axis=2)
            return pats
        k, gc = (3, 16)
        b, _, h, w = x.shape
        cmid = w1.shape[0]
        G = w2.shape[0] // (k * k)
        t = jax.nn.relu(group_norm(d4_1x1(x, w1), gn_gamma, gn_beta, cmid))
        tr = t.reshape(b, cmid, 8, h, w)
        wgt = jnp.einsum('oi,bighw->boghw', w2, tr) + b2[None, :, None, None, None]
        wv = wgt.reshape(b, G, k, k, 8, h, w)
        s = [wv[:, :, :, :, g] for g in range(8)]
        sw = [jnp.swapaxes(s[g], 2, 3) for g in range(4, 8)]
        trans = [s[0], jnp.rot90(s[1], 1, (2, 3)), jnp.rot90(s[2], 2, (2, 3)), jnp.rot90(s[3], 3, (2, 3)), jnp.rot90(sw[0], 3, (2, 3)), jnp.rot90(sw[1], 2, (2, 3)), jnp.rot90(sw[2], 1, (2, 3)), sw[3]]
        wv = jnp.stack(trans, axis=4)
        wv = wv.reshape(b, G, k * k, 8, h, w)[:, :, None]
        wv = jnp.swapaxes(wv, 3, 4)
        xv = d4_1x1(x, w_v)
        pats = unfold_patches(xv, k).reshape(b, G, gc, 8, k * k, h, w)
        out = (wv * pats).sum(axis=4)
        return out.reshape(b, G * gc * 8, h, w)

    def _gn(v, G=32, eps=1e-5):
        B_, C_, H_, W_ = v.shape
        g = v.reshape(B_, G, C_ // G, H_, W_)
        m = jnp.mean(g, axis=(2, 3, 4), keepdims=True)
        s = jnp.var(g, axis=(2, 3, 4), keepdims=True)
        return ((g - m) / jnp.sqrt(s + eps)).reshape(v.shape)

    def _ln_c(v, eps=1e-6):
        m = jnp.mean(v, axis=1, keepdims=True)
        s = jnp.var(v, axis=1, keepdims=True)
        return (v - m) / jnp.sqrt(s + eps)

    def _ln_t(v, eps=1e-5):
        m = jnp.mean(v, axis=-1, keepdims=True)
        s = jnp.var(v, axis=-1, keepdims=True)
        return (v - m) / jnp.sqrt(s + eps)

    def _to_tokens(v):
        B_, C_, H_, W_ = v.shape
        return v.reshape(B_, C_, H_ * W_).transpose(0, 2, 1)
    def _from_tokens(t, like):
        B_, C_, H_, W_ = like.shape
        return t.transpose(0, 2, 1).reshape(B_, C_, H_, W_)

    x = x + _L0_conv_ref(_gn(x), L0_conv_kernel)
    x = x + _L1_conv_ref(_gn(x), L1_conv_w_v, L1_conv_w1, L1_conv_gn_gamma, L1_conv_gn_beta, L1_conv_w2, L1_conv_b2)
    return x


_drawn_inputs = setup_inputs


def setup_inputs(seed=0):
    import zlib

    import numpy as np

    out = dict(_drawn_inputs(seed))
    spreads = {'L1_conv_gn_gamma': (1.0, 0.2), 'L1_conv_gn_beta': (0.0, 0.1), 'L1_conv_b2': (0.0, 0.1)}
    factors = {}
    for name, (base, spread) in spreads.items():
        noise = np.random.default_rng([zlib.crc32(name.encode()), seed]).standard_normal(out[name].shape)
        drawn = base * np.exp(spread * noise) if base else spread * noise
        out[name] = jnp.asarray(drawn.astype(out[name].dtype))
    for name, factor in factors.items():
        out[name] = (out[name] * factor).astype(out[name].dtype)
    return out
```

```python
from contextlib import ExitStack

import concourse.bass as bass
from concourse import mybir

F32 = mybir.dt.float32
ALU = mybir.AluOpType
ACT = mybir.ActivationFunctionType
AX_X = mybir.AxisListType.X

P = 128
B, C, H, W = 16, 512, 64, 64
HW = H * W
CG, CM, GR = 4, 16, 8
EPS = 1e-5

STEPS = CM // 2
GPS = CG
PAIRS = 2 * CG * GR // 2
TAPS0 = 4
XP = 68
X_RING, N_RING = 4, 2

BANDS = 4
UNITS, UR = 4, 4
UPX = UR * W
KT = C // P
CMID = 32 * GR
MT = CMID // P
TAPS1 = 9
QM = 4
GRANS = CM // QM
VP = W + 2
HALO0 = 7
ROWS = [7, 4, 4, 3]
POOL_TAPS = [3, 4, 5, 6, 7, 8]
DVE_TAPS = [0, 1, 2]
TAP_ORDER = [3, 0, 4, 1, 5, 6, 2, 7, 8]
NPT = len(POOL_TAPS)
WV_BANKS = 5
ACC_RING = 4


def wait_apart(engine, apart, sem, value):
    engine.wait_ge(sem, value)
    engine.sem_inc(apart, 1)


def program(nc, x, shifts, mean_a, kern, member_of, w1t, wvt, w2t, w2mask, b2t, gamma, beta, mean_b, out, x1):
    with ExitStack() as top:
        def sem(name, ctx=top):
            return ctx.enter_context(nc.semaphore(name))

        ps = top.enter_context(nc.psum_tensor("ps", [P, 8, 512], F32))
        x1_scale = top.enter_context(nc.sbuf_tensor("x1_scale", [P, B * KT], F32))
        x1_bias = top.enter_context(nc.sbuf_tensor("x1_bias", [P, B * KT], F32))
        with ExitStack() as ctx:
            stage_a(nc, ctx, sem, ps, x, shifts, mean_a, kern, member_of, x1, x1_scale, x1_bias)
        with ExitStack() as ctx:
            stage_b(nc, ctx, sem, ps, x1, w1t, wvt, w2t, w2mask, b2t, gamma, beta, mean_b, out, x1_scale, x1_bias)


def stage_a(nc, ctx, sem, ps, x, shifts, mean_a, kern, member_of, x1, x1_scale, x1_bias):
    def sb(name, shape):
        return ctx.enter_context(nc.sbuf_tensor(name, shape, F32))

    NS = B * STEPS
    x_in = sb("x_in", [P, X_RING, PAIRS * W])
    x_out = sb("x_out", [P, X_RING, PAIRS * W])
    xn = sb("xn", [P, N_RING, PAIRS * XP])
    shift_m = sb("shift_m", [P, TAPS0, P])
    band = sb("band", [P, TAPS0, P])
    kern_b = sb("kern_b", [P, TAPS0 * TAPS0])
    ones = sb("ones", [P, P])
    member = sb("member", [P, 2 * CG])
    power = sb("power", [P, GPS])
    table_s = sb("table_s", [P, B, STEPS * GPS])
    table_b = sb("table_b", [P, B, STEPS * GPS])
    pick = sb("pick", [P, B * KT, 2 * CG])
    six = [sb(f"six{j}", [P, GPS, 6]) for j in range(2)]
    mv = [sb(f"mv{j}", [P, GPS, 2]) for j in range(2)]
    dev = [sb(f"dev{j}", [P, GPS]) for j in range(2)]
    spread = [sb(f"spread{j}", [P, GPS]) for j in range(2)]
    var_eps = [sb(f"var_eps{j}", [P, GPS]) for j in range(2)]
    norm_s = sb("norm_s", [P, N_RING, GPS])
    norm_b = sb("norm_b", [P, N_RING, GPS])

    const_in = sem("a_const_in")
    sp_apart, dve_apart = sem("a_sp_apart"), sem("a_dve_apart")
    setup = sem("a_setup")
    band_built = sem("band_built")
    x_loaded = [sem(f"x_loaded{r}") for r in range(X_RING)]
    x1_stored = [sem(f"x1_stored{r}") for r in range(X_RING)]
    x_added = sem("x_added")
    xn_ready = sem("xn_ready")
    blurred = sem("blurred")
    norm_ready = sem("norm_ready")
    local_done = [sem(f"local_done{j}") for j in range(2)]
    mean_done = [sem(f"mean_done{j}") for j in range(2)]
    spread_done = [sem(f"spread_done{j}") for j in range(2)]
    var_done = [sem(f"var_done{j}") for j in range(2)]
    var_eps_done = [sem(f"var_eps_done{j}") for j in range(2)]
    rstd_done = [sem(f"rstd_done{j}") for j in range(2)]
    stats_chain = [sem(f"stats_chain{j}") for j in range(2)]
    table_done = sem("table_done")
    picked = sem("picked")

    MEAN_BANK, VAR_BANK = [4, 6], [5, 7]

    def group(buf, pitch, width, lo, g):
        return buf.rearrange("p (m c h w) -> p m c h w", m=2, c=CG, w=pitch)[:, :, g, :, lo:lo + width]


    def where(i, k):
        return i + k // STEPS, k % STEPS

    block = ctx.enter_context(nc.Block())

    @block.sync
    def _(sp):
        sp.dma_start(shift_m[:], shifts).then_inc(const_in, 16)
        sp.dma_start(ones[:], mean_a).then_inc(const_in, 16)
        sp.dma_start(kern_b[:], kern.partition_broadcast(P)).then_inc(const_in, 16)
        sp.dma_start(member[:], member_of).then_inc(const_in, 16)

        def load(i, k):
            img, s = where(i, k)
            sp.dma_start(x_in[:, k % X_RING, :], x[img, s]).then_inc(x_loaded[k % X_RING], 16)

        def store(i, k):
            img, s = where(i, k)
            src = x_out[:, k % X_RING, :].rearrange("p (m a w) -> p m a w", m=2, w=W)
            for m in range(2):
                dst = x1[img, (2 * s + m) * 32:(2 * s + m + 1) * 32].rearrange("(a t) h w -> (t h) a w", t=2)
                sp.dma_start(dst, src[:, m]).then_inc(x1_stored[k % X_RING], 16)

        def slot(i, k, first=False, last=False):
            if not first:
                wait_apart(sp, sp_apart, x_added, i * (STEPS * GPS) + GPS * (k - X_RING + 1))
                store(i, k - X_RING)
            if not last:
                load(i, k)

        for k in range(X_RING):
            slot(0, k, first=True)
        with sp.Fori(0, B - 1) as i:
            for k in range(X_RING, X_RING + STEPS):
                slot(i, k)
        for k in range(X_RING, X_RING + STEPS):
            slot(B - 1, k, last=k >= STEPS)
        for r in range(X_RING):
            sp.wait_ge(x1_stored[r], 32 * (NS // X_RING))

    @block.scalar
    def _(act):
        def slot(i, k):
            r = k % N_RING
            act.wait_ge(norm_ready, i * STEPS + k + 1)
            if not (isinstance(i, int) and i == 0 and k < N_RING):
                act.wait_ge(blurred, i * (STEPS * GPS) + GPS * (k - N_RING + 1))
            for g in range(GPS):
                nc.scalar.activation(group(xn[:, r, :], XP, W, 2, g), group(x_in[:, k % X_RING, :], W, W, 0, g),
                                     ACT.Identity, bias=norm_b[:, r, g:g + 1],
                                     scale=norm_s[:, r, g:g + 1]).then_inc(xn_ready, 1)
        act.wait_ge(setup, 2)
        slot(0, 0)
        slot(0, 1)
        with act.Fori(0, B - 1) as i:
            for k in range(2, 2 + STEPS):
                slot(i, k)
        for k in range(2, STEPS):
            slot(B - 1, k)

    @block.tensor
    def _(pe):
        def mean_over_partitions(i, k, j):
            pe.wait_ge(local_done[j], i * STEPS + k + 1)
            nc.tensor.matmul(ps[:, MEAN_BANK[j], 0:GPS], ones[:], mv[j][:, :, 0], start=True, stop=True)\
                .then_inc(mean_done[j], 1)

        def var_over_partitions(i, k, j):
            pe.wait_ge(spread_done[j], i * STEPS + k + 1)
            nc.tensor.matmul(ps[:, VAR_BANK[j], 0:GPS], ones[:], spread[j][:], start=True, stop=True)\
                .then_inc(var_done[j], 1)

        def blur(i, k, g):
            n = i * (STEPS * GPS) + GPS * k + g
            pe.wait_ge(xn_ready, n + 1)
            if not (isinstance(i, int) and i == 0 and k < 1):
                pe.wait_ge(x_added, n - GPS + 1)
            for v in range(TAPS0):
                mm = nc.tensor.matmul(ps[:, g, :], band[:, v, :], group(xn[:, k % N_RING, :], XP, W, v, g),
                                      start=(v == 0), stop=(v == TAPS0 - 1))
            mm.then_inc(blurred, 1)

        def slot(i, k, first=1, last=0):
            if first >= 1 and last < 2 and not (first == 1 and k == 0):
                blur(i, k - 1, 0)
            if last < 1:
                mean_over_partitions(i, k, 0)
            if last < 2 and k >= 1:
                blur(i, k - 1, 1)
            if last < 1:
                var_over_partitions(i, k, 0)
            if last < 2 and k >= 1:
                blur(i, k - 1, 2)
            if k >= 2:
                mean_over_partitions(i, k - 2, 1)
            if last < 2 and k >= 1:
                blur(i, k - 1, 3)
            if k >= 2:
                var_over_partitions(i, k - 2, 1)

        pe.wait_ge(band_built, TAPS0)
        slot(0, 0)
        slot(0, 1)
        with pe.Fori(0, B - 1) as i:
            for k in range(2, 2 + STEPS):
                slot(i, k)
        for k in range(2, STEPS):
            slot(B - 1, k)
        slot(B - 1, STEPS, last=1)
        slot(B - 1, STEPS + 1, last=2)

    @block.gpsimd
    def _(pool):
        nc.gpsimd.memset(xn[:], 0.0).then_inc(setup, 1)
        nc.gpsimd.memset(power[:], -0.5).then_inc(setup, 1)
        pool.wait_ge(setup, 2)

        def slot(i, k, x_step=True, x1_step=True):
            if x_step:
                pool.wait_ge(var_eps_done[0], i * STEPS + k + 1)
                nc.gpsimd.tensor_tensor(norm_s[:, k % N_RING, :], var_eps[0][:], power[:], ALU.pow)\
                    .then_inc(rstd_done[0], 1)
            if x1_step:
                img, s = where(i, k - 2)
                pool.wait_ge(var_eps_done[1], i * STEPS + k - 1)
                nc.gpsimd.tensor_tensor(table_s[:, img, s * GPS:(s + 1) * GPS], var_eps[1][:], power[:], ALU.pow)\
                    .then_inc(rstd_done[1], 1)

        slot(0, 0, x1_step=False)
        slot(0, 1, x1_step=False)
        with pool.Fori(0, B - 1) as i:
            for k in range(2, 2 + STEPS):
                slot(i, k)
        for k in range(2, STEPS + 2):
            slot(B - 1, k, x_step=k < STEPS)

    @block.vector
    def _(dve):
        LOCAL, CHAIN = 1, 3

        def chain_at(i, k, n):
            return i * (STEPS * CHAIN) + CHAIN * k + n

        def local_stats(i, k, j, buf):
            for g in range(GPS):
                src = buf.rearrange("p (m c w) -> p m c w", m=2, c=CG)[:, :, g, :]
                last = nc.vector.bn_stats(six[j][:, g, :], src)
            last.then_inc(stats_chain[j], 1)
            wait_apart(dve, dve_apart, stats_chain[j], chain_at(i, k, 1))
            for g in range(GPS):
                last = nc.vector.bn_aggr(mv[j][:, g, :], six[j][:, g, :])
            last.then_inc(local_done[j], 1)

        def spreads(i, k, j):
            dve.wait_ge(local_done[j], i * STEPS + k + 1)
            dve.wait_ge(mean_done[j], i * STEPS + k + 1)
            nc.vector.tensor_tensor(dev[j][:], mv[j][:, :, 0], ps[:, MEAN_BANK[j], 0:GPS], ALU.subtract)\
                .then_inc(stats_chain[j], 1)
            dve.wait_ge(stats_chain[j], chain_at(i, k, 2))
            nc.vector.tensor_tensor(dev[j][:], dev[j][:], dev[j][:], ALU.mult).then_inc(stats_chain[j], 1)
            dve.wait_ge(stats_chain[j], chain_at(i, k, 3))
            nc.vector.tensor_tensor(spread[j][:], dev[j][:], mv[j][:, :, 1], ALU.add).then_inc(spread_done[j], 1)

        def add_eps(i, k, j):
            dve.wait_ge(var_done[j], i * STEPS + k + 1)
            nc.vector.tensor_scalar(var_eps[j][:], ps[:, VAR_BANK[j], 0:GPS], EPS, None, ALU.add)\
                .then_inc(var_eps_done[j], 1)

        def offset(i, k, j, rstd, dst, done):
            dve.wait_ge(rstd_done[j], i * STEPS + k + 1)
            nc.vector.scalar_tensor_tensor(out=dst, in0=ps[:, MEAN_BANK[j], 0:GPS], scalar=-1.0, in1=rstd,
                                           op0=ALU.mult, op1=ALU.mult).then_inc(done, 1)

        def add_x(i, k, g):
            r = k % X_RING
            dve.wait_ge(blurred, i * (STEPS * GPS) + GPS * k + g + 1)
            if g == 0 and not (isinstance(i, int) and i == 0 and k < X_RING):
                dve.wait_ge(x1_stored[r], i * (32 * STEPS // X_RING) + 32 * (k // X_RING))
            nc.vector.tensor_tensor(group(x_out[:, r, :], W, W, 0, g).rearrange("p m h w -> p m (h w)"),
                                    ps[:, g, :].rearrange("p (m n) -> p m n", m=2),
                                    group(x_in[:, r, :], W, W, 0, g).rearrange("p m h w -> p m (h w)"),
                                    ALU.add).then_inc(x_added, 1)

        def slot(i, k, now=True, prev=True, prev2=True):
            if now:
                dve.wait_ge(x_loaded[k % X_RING], i * (16 * STEPS // X_RING) + 16 * (k // X_RING + 1))
                local_stats(i, k, 0, x_in[:, k % X_RING, :])
            if prev:
                add_x(i, k - 1, 0)
            if now:
                spreads(i, k, 0)
            if prev:
                add_x(i, k - 1, 1)
            if now:
                add_eps(i, k, 0)
            if prev:
                add_x(i, k - 1, 2)
            if now:
                offset(i, k, 0, norm_s[:, k % N_RING, :], norm_b[:, k % N_RING, :], norm_ready)
            if prev2:
                spreads(i, k - 2, 1)
            if prev:
                add_x(i, k - 1, 3)
            if prev2:
                img, s = where(i, k - 2)
                add_eps(i, k - 2, 1)
                offset(i, k - 2, 1, table_s[:, img, s * GPS:(s + 1) * GPS], table_b[:, img, s * GPS:(s + 1) * GPS],
                       table_done)
            if prev:
                dve.wait_ge(x_added, i * (STEPS * GPS) + GPS * k)
                local_stats(i, k - 1, 1, x_out[:, (k - 1) % X_RING, :])

        dve.wait_ge(const_in, 64)
        for v in range(TAPS0):
            for u in range(TAPS0):
                j = (TAPS0 - 1 - u) * TAPS0 + TAPS0 - 1 - v
                if u == 0:
                    last = nc.vector.tensor_scalar(band[:, v, :], shift_m[:, u, :], kern_b[:, j:j + 1], None, ALU.mult)
                else:
                    dve.wait_ge(picked, v * (TAPS0 - 1) + u)
                    last = nc.vector.scalar_tensor_tensor(out=band[:, v, :], in0=shift_m[:, u, :],
                                                          scalar=kern_b[:, j:j + 1], in1=band[:, v, :],
                                                          op0=ALU.mult, op1=ALU.add)
                last.then_inc(picked if u < TAPS0 - 1 else band_built, 1)
        slot(0, 0, prev=False, prev2=False)
        slot(0, 1, prev2=False)
        with dve.Fori(0, B - 1) as i:
            for k in range(2, 2 + STEPS):
                slot(i, k)
        for k in range(2, STEPS + 2):
            slot(B - 1, k, now=k < STEPS, prev=k < STEPS + 1)
        n = TAPS0 * (TAPS0 - 1)
        dve.wait_ge(table_done, NS)
        for table, dst in ((table_s, x1_scale), (table_b, x1_bias)):
            nc.vector.tensor_tensor(pick[:], table[:].rearrange("p b (t e) -> p (b t) e", e=2 * CG),
                                    member[:].unsqueeze(1).to_broadcast([P, B * KT, 2 * CG]), ALU.mult)\
                .then_inc(picked, 1)
            n += 1
            dve.wait_ge(picked, n)
            nc.vector.tensor_reduce(dst[:], pick[:], AX_X, ALU.add).then_inc(picked, 1)
            n += 1
            dve.wait_ge(picked, n)


def stage_b(nc, ctx, sem, ps, x1, w1t, wvt, w2t, w2mask, b2t, gamma, beta, mean_b, out, x1_scale, x1_bias):
    def sb(name, shape):
        return ctx.enter_context(nc.sbuf_tensor(name, shape, F32))

    xm = sb("xm", [P, KT, (H + 2) * W])
    t = sb("t", [P, MT, UNITS, BANDS * UPX])
    val = [sb("val0", [P, CM, HALO0, VP]), sb("val1", [P, CM, UR + 2, VP])]
    acc_p = sb("acc_p", [P, ACC_RING, QM * UPX])
    acc_d = sb("acc_d", [P, 2, QM * UPX])
    prod_p = sb("prod_p", [P, 2, QM * UPX])
    prod_d = sb("prod_d", [P, 2, QM * UPX])
    w1 = sb("w1", [P, KT, CMID])
    wv = sb("wv", [P, KT, CM * 32])
    w2 = sb("w2", [P, MT, TAPS1 * 32])
    blk = sb("blk", [P, P])
    b2 = sb("b2", [P, TAPS1])
    gam = sb("gam", [P, MT])
    bet = sb("bet", [P, MT])
    power = sb("power_b", [P, MT])
    six = sb("six_t", [P, MT, 2 * UNITS, 6])
    mv = sb("mv_t", [P, MT, 2])
    dev = sb("dev_t", [P, MT])
    spread = sb("spread_t", [P, MT])
    var_eps = sb("var_eps_t", [P, MT])
    rstd = sb("rstd_t", [P, MT])
    t_scale = sb("t_scale", [P, MT])
    t_bias = sb("t_bias", [P, MT])
    mask = prod_d[:, 0, 0:TAPS1 * 32]

    const_in = sem("b_const_in")
    sp_apart, act_apart, dve_apart = sem("b_sp_apart"), sem("b_act_apart"), sem("b_dve_apart")
    setup = sem("b_setup")
    w2_built = sem("w2_built")
    xm_loaded = [sem(f"xm_loaded{u}") for u in range(UNITS)]
    xm_ready = sem("xm_ready")
    mm_full = sem("mm_full")
    kept = sem("kept")
    halo_ready = sem("halo_ready")
    t_ready = sem("t_ready")
    tap_mm = sem("tap_mm")
    tap_ready = sem("tap_ready")
    prod_ready = sem("prod_ready")
    prod_added = sem("prod_added")
    own = sem("own")
    summed = sem("summed")
    resid_in = [sem(f"resid_in{r}") for r in range(ACC_RING)]
    stored = [sem(f"stored{r}") for r in range(ACC_RING)]
    t_chain = sem("t_chain")
    t_local, t_mean, t_spread, t_var, t_var_eps, t_rstd, t_norm = (
        sem(n) for n in ("t_local", "t_mean", "t_spread", "t_var", "t_var_eps", "t_rstd", "t_norm"))

    TAP0, RING0, STAT_BANK = 0, WV_BANKS, 7
    N_GRAN = UNITS * GRANS
    HALOS = [0, 1, 2, 4]
    LEAD_MM, PERIOD_MM = 16 + 16, 16 + 40
    OWN = 5
    bank_of = {tap: TAP0 + n // 2 for n, tap in enumerate(TAP_ORDER)}
    half_of = {tap: n % 2 for n, tap in enumerate(TAP_ORDER)}
    banks = [TAP_ORDER[2 * b:2 * b + 2] for b in range(WV_BANKS)]

    def taps_of(tap):
        return ps[:, bank_of[tap], half_of[tap] * UPX:(half_of[tap] + 1) * UPX]


    def values_at(i, u, j, more):
        if u == 0:
            return i * PERIOD_MM + LEAD_MM - 16 + j
        return i * PERIOD_MM + LEAD_MM + (12 if more else 8) * (u - 1) + j

    def t_at(i, u):
        if isinstance(i, int) and i == 0:
            return 4 * u
        return i * PERIOD_MM + LEAD_MM - PERIOD_MM + (8, 20, 32, 36)[u]

    def product_done(i, n, tap):
        if tap in POOL_TAPS:
            return prod_ready, i * (NPT * N_GRAN) + NPT * n + [t for t in TAP_ORDER if t in POOL_TAPS].index(tap) + 1
        return own, i * (OWN * N_GRAN) + OWN * n + {0: 1, 1: 2, 2: 4}[tap]

    def unit_done(i, u):
        return product_done(i, GRANS * u + GRANS - 1, TAP_ORDER[-1])

    def first(i, k=0):
        return isinstance(i, int) and i == 0 and k <= 0

    block = ctx.enter_context(nc.Block())

    @block.sync
    def _(sp):
        for dst, src in ((w1, w1t), (wv, wvt), (w2, w2t), (blk, mean_b), (b2, b2t), (gam, gamma), (bet, beta)):
            sp.dma_start(dst[:], src).then_inc(const_in, 16)
        sp.dma_start(mask, w2mask).then_inc(const_in, 16)

        def load_xm(i, u):
            if not first(i):
                wait_apart(sp, sp_apart, mm_full, values_at(i - 1, u, 16 if u == 0 else 8, True))
            for kt in range(KT):
                dst = xm[:, kt, :].rearrange("p (r w) -> p r w", w=W)[:, 1:1 + H, :]\
                    .rearrange("p (q r) w -> p q (r w)", q=BANDS)[:, :, u * UPX:(u + 1) * UPX]
                src = x1[i, kt * P:(kt + 1) * P].rearrange("c (q r) w -> c q (r w)", q=BANDS)[
                    :, :, u * UPX:(u + 1) * UPX]
                sp.dma_start(dst, src).then_inc(xm_loaded[u], 16)

        def load_resid(i, n):
            u, q4, r = (n // GRANS) % UNITS, n % GRANS, n % ACC_RING
            if not first(i, n - ACC_RING + 1):
                wait_apart(sp, sp_apart, stored[r], i * (16 * N_GRAN // ACC_RING) + 16 * (n // ACC_RING))
            img = i + n // N_GRAN
            for q in range(BANDS):
                src = x1[img].rearrange("(m e) h w -> e m (h w)", m=CM)[
                    :, q4 * QM:(q4 + 1) * QM, (q * 16 + u * UR) * W:(q * 16 + (u + 1) * UR) * W]
                dst = acc_p[32 * q:32 * q + 32, r, :].rearrange("p (m n) -> p m n", m=QM)
                sp.dma_start(dst, src).then_inc(resid_in[r], 16)

        def store(i, n):
            wait_apart(sp, sp_apart, summed, i * N_GRAN + n + 1)
            img, m = (i + n // N_GRAN, n % N_GRAN) if n >= 0 else (i - 1, n + N_GRAN)
            sp.dma_start(out[img, m], acc_p[:, n % ACC_RING, :]).then_inc(stored[n % ACC_RING], 16)

        LOAD_AT = {2: 0, 5: 1, 9: 2, 12: 3}
        for u in range(UNITS):
            load_xm(0, u)
        load_resid(0, 0)
        load_resid(0, 1)

        def period(i, lead=True, begin=False):
            for n in range(N_GRAN):
                if lead and n in LOAD_AT:
                    load_xm(i + 1, LOAD_AT[n])
                if lead or n + 2 < N_GRAN:
                    load_resid(i, n + 2)
                if not (begin and n == 0):
                    store(i, n - 1)

        period(0, begin=True)
        with sp.Fori(1, B - 1) as i:
            period(i)
        period(B - 1, lead=False)
        store(B - 1, N_GRAN - 1)
        for r in range(ACC_RING):
            sp.wait_ge(stored[r], 16 * B * N_GRAN // ACC_RING)

    @block.tensor
    def _(pe):
        class Ring:
            base, n = 0, 0

        def bank():
            return RING0 + Ring.n % 2

        def take():
            if not (isinstance(Ring.base, int) and Ring.base == 0 and Ring.n < 2):
                pe.wait_ge(kept, Ring.base + Ring.n - 1)
            return bank()

        def conv_t(i, u):
            pe.wait_ge(xm_ready, i * (KT * UNITS) + KT * (u + 1))
            for m in range(MT):
                for h in range(2):
                    b = take()
                    for kt in range(KT):
                        rhs = xm[:, kt, W:W + HW].rearrange("p (q n) -> p q n", q=BANDS)[
                            :, 2 * h:2 * h + 2, u * UPX:(u + 1) * UPX]
                        mm = nc.tensor.matmul(ps[:, b, :], w1[:, kt, m * P:(m + 1) * P], rhs,
                                              start=(kt == 0), stop=(kt == KT - 1))
                    mm.then_inc(mm_full, 1)
                    Ring.n += 1

        def values(i, u, members):
            per = 1 if u == 0 else 2
            for m0 in members[::per]:
                b = take()
                for j in range(per):
                    parts = [(-1, 6), (16, 1)] if u == 0 else [(u * UR + 1, ROWS[u])]
                    at = j * ROWS[u] * W
                    for row, n in parts:
                        for kt in range(KT):
                            for q in range(BANDS):
                                r0 = (1 + 16 * q + row) * W
                                mm = nc.tensor.matmul(ps[32 * q:32 * q + 32, b, at:at + n * W],
                                                      wv[:, kt, (m0 + j) * 32:(m0 + j + 1) * 32],
                                                      xm[:, kt, r0:r0 + n * W],
                                                      start=(kt == 0), stop=(kt == KT - 1),
                                                      skip_group_check=True)
                        at += n * W
                mm.then_inc(mm_full, 1)
                Ring.n += 1

        def tap_weights(i, u):
            pe.wait_ge(t_ready, i * (MT * UNITS) + MT * (u + 1))
            for b in range(WV_BANKS):
                if not first(i, u):
                    pe.wait_ge(*product_done(i, GRANS * u - 1, banks[b][-1]))
                for tap in banks[b]:
                    for kt in range(MT):
                        for q in range(BANDS):
                            mm = nc.tensor.matmul(taps_of(tap)[32 * q:32 * q + 32, :],
                                                  w2[:, kt, tap * 32:(tap + 1) * 32],
                                                  t[:, kt, u, q * UPX:(q + 1) * UPX],
                                                  start=(kt == 0), stop=(kt == MT - 1),
                                                  skip_group_check=True)
                mm.then_inc(tap_mm, 1)

        def lead(i):
            conv_t(i, 3)
            values(i, 0, range(0, 4))
            pe.wait_ge(t_local, i + 1)
            nc.tensor.matmul(ps[:, STAT_BANK, 0:MT], blk[:], mv[:, :, 0], start=True, stop=True).then_inc(t_mean, 1)
            values(i, 0, range(4, 7))
            pe.wait_ge(t_spread, i + 1)
            nc.tensor.matmul(ps[:, STAT_BANK, 8:8 + MT], blk[:], spread[:], start=True, stop=True)\
                .then_inc(t_var, 1)
            values(i, 0, range(7, 10))
            tap_weights(i, 0)
            values(i, 0, range(10, 16))

        pe.wait_ge(const_in, 16 * 8)
        pe.wait_ge(setup, 4)
        for u in range(3):
            conv_t(0, u)
        pe.wait_ge(w2_built, 1)
        lead(0)

        def period(i, more=True):
            Ring.base, Ring.n = i * PERIOD_MM, LEAD_MM
            for u in range(3):
                if u > 0:
                    tap_weights(i, u)
                values(i, u + 1, range(CM))
                if more:
                    conv_t(i + 1, u)
            tap_weights(i, 3)
            if more:
                lead(i + 1)

        period(0)
        with pe.Fori(1, B - 1) as i:
            period(i)
        period(B - 1, more=False)

    @block.scalar
    def _(act):
        class Ring:
            base, n = 0, 0

        def take():
            act.wait_ge(mm_full, Ring.base + Ring.n + 1)
            b = RING0 + Ring.n % 2
            Ring.n += 1
            return b

        def normalize(i, u):
            wait_apart(act, act_apart, xm_loaded[u], i * (16 * KT) + 16 * KT)
            for kt in range(KT):
                v = xm[:, kt, W:W + HW].rearrange("p (q n) -> p q n", q=BANDS)[:, :, u * UPX:(u + 1) * UPX]
                nc.scalar.activation(v, v, ACT.Identity, bias=x1_bias[:, bass.ds(i * KT + kt, 1)],
                                     scale=x1_scale[:, bass.ds(i * KT + kt, 1)]).then_inc(xm_ready, 1)

        def keep_t(i, u):
            for m in range(MT):
                for h in range(2):
                    b = take()
                    nc.scalar.activation(t[:, m, u, 512 * h:512 * (h + 1)], ps[:, b, :], ACT.Copy)\
                        .then_inc(kept, 1)

        def halos(i, u, more):
            if not first(i, u - 1):
                act.wait_ge(*unit_done(i, u - 2))
            act.wait_ge(kept, values_at(i, u - 1, 16 if u == 1 else 8, more))
            src, dst = val[(u - 1) % 2], val[u % 2]
            nc.scalar.activation(dst[:, :, 0:2, 1:1 + W], src[:, :, 4:6, 1:1 + W], ACT.Copy).then_inc(halo_ready, 1)
            if u == 3:
                nc.scalar.activation(dst[:, :, 5, 1:1 + W], src[:, :, 6, 1:1 + W], ACT.Copy).then_inc(halo_ready, 1)

        def keep_values(i, u, members):
            per = 1 if u == 0 else 2
            if u == 0 and members[0] == 0 and not first(i):
                act.wait_ge(*unit_done(i - 1, 2))
                act.wait_ge(halo_ready, i * HALOS[3])
            for m0 in members[::per]:
                b = take()
                src = ps[:, b, 0:per * ROWS[u] * W].rearrange("p (m r w) -> p m r w", m=per, w=W)
                lo = 0 if u == 0 else 2
                nc.scalar.activation(val[u % 2][:, m0:m0 + per, lo:lo + ROWS[u], 1:1 + W], src, ACT.Copy)\
                    .then_inc(kept, 1)

        def tap_bias(i, u):
            for b in range(WV_BANKS):
                act.wait_ge(tap_mm, i * (UNITS * WV_BANKS) + WV_BANKS * u + b + 1)
                for tap in banks[b]:
                    last = nc.scalar.activation(taps_of(tap), taps_of(tap), ACT.Identity, bias=b2[:, tap:tap + 1])
                last.then_inc(tap_ready, 1)

        def relu(i, u):
            act.wait_ge(t_norm, i + 1)
            for m in range(MT):
                nc.scalar.activation(t[:, m, u, :], t[:, m, u, :], ACT.Relu, bias=t_bias[:, m:m + 1],
                                     scale=t_scale[:, m:m + 1]).then_inc(t_ready, 1)

        def lead(i):
            normalize(i, 3)
            keep_t(i, 3)
            keep_values(i, 0, range(0, 8))
            relu(i, 0)
            keep_values(i, 0, range(8, 10))
            tap_bias(i, 0)
            keep_values(i, 0, range(10, 16))
            for u in range(1, UNITS):
                relu(i, u)

        act.wait_ge(const_in, 16 * 8)
        act.wait_ge(setup, 4)
        for u in range(3):
            normalize(0, u)
            keep_t(0, u)
        lead(0)

        def period(i, more=True):
            Ring.base, Ring.n = i * PERIOD_MM, LEAD_MM
            for u in range(3):
                if u > 0:
                    tap_bias(i, u)
                halos(i, u + 1, more)
                keep_values(i, u + 1, range(0, 8))
                if more:
                    normalize(i + 1, u)
                keep_values(i, u + 1, range(8, 16))
                if more:
                    keep_t(i + 1, u)
            tap_bias(i, 3)
            if more:
                lead(i + 1)

        period(0)
        with act.Fori(1, B - 1) as i:
            period(i)
        period(B - 1, more=False)

    @block.gpsimd
    def _(pool):
        nc.gpsimd.memset(xm[:, :, 0:W], 0.0).then_inc(setup, 1)
        nc.gpsimd.memset(xm[:, :, W + HW:], 0.0).then_inc(setup, 1)
        nc.gpsimd.memset(power[:], -0.5).then_inc(setup, 1)
        nc.gpsimd.memset(val[0][:], 0.0)
        nc.gpsimd.memset(val[1][:], 0.0).then_inc(setup, 1)
        pool.wait_ge(setup, 4)

        def t_rstd_of(i):
            pool.wait_ge(t_var_eps, i + 1)
            nc.gpsimd.tensor_tensor(rstd[:], var_eps[:], power[:], ALU.pow).then_inc(t_rstd, 1)

        t_rstd_of(0)

        def period(i, more=True):
            for n in range(N_GRAN):
                r = n % ACC_RING
                pool.wait_ge(resid_in[r], i * (64 * N_GRAN // ACC_RING) + 64 * (n // ACC_RING + 1))
                for j in range(NPT):
                    k = NPT * n + j
                    pool.wait_ge(prod_ready, i * (NPT * N_GRAN) + k + 1)
                    if not first(i, k):
                        pool.wait_ge(prod_added, i * (NPT * N_GRAN) + k)
                    nc.gpsimd.tensor_tensor(acc_p[:, r, :], acc_p[:, r, :], prod_p[:, k % 2, :], ALU.add)\
                        .then_inc(prod_added, 1)
                    if more and n == N_GRAN - 1 and j == 1:
                        t_rstd_of(i + 1)

        period(0)
        with pool.Fori(1, B - 1) as i:
            period(i)
        period(B - 1, more=False)

    @block.vector
    def _(dve):
        def t_stats(i, u):
            dve.wait_ge(kept, t_at(i, u) + 4)
            for m in range(MT):
                for h in range(2):
                    last = nc.vector.bn_stats(six[:, m, 2 * u + h, :], t[:, m, u, 512 * h:512 * (h + 1)])
            last.then_inc(t_chain, 1)

        CH = UNITS + 4

        def t_aggregate(i):
            wait_apart(dve, dve_apart, t_chain, i * CH + UNITS)
            for m in range(MT):
                last = nc.vector.bn_aggr(mv[:, m, :], six[:, m, :, :].rearrange("p a b -> p (a b)"))
            last.then_inc(t_local, 1)

        def t_spreads(i):
            dve.wait_ge(t_local, i + 1)
            dve.wait_ge(t_mean, i + 1)
            nc.vector.tensor_tensor(dev[:], mv[:, :, 0], ps[:, STAT_BANK, 0:MT], ALU.subtract).then_inc(t_chain, 1)
            dve.wait_ge(t_chain, i * CH + UNITS + 1)
            nc.vector.tensor_tensor(dev[:], dev[:], dev[:], ALU.mult).then_inc(t_chain, 1)
            dve.wait_ge(t_chain, i * CH + UNITS + 2)
            nc.vector.tensor_tensor(spread[:], dev[:], mv[:, :, 1], ALU.add).then_inc(t_spread, 1)

        def t_add_eps(i):
            dve.wait_ge(t_var, i + 1)
            nc.vector.tensor_scalar(var_eps[:], ps[:, STAT_BANK, 8:8 + MT], EPS, None, ALU.add)\
                .then_inc(t_var_eps, 1)

        def t_affine(i):
            dve.wait_ge(t_rstd, i + 1)
            nc.vector.tensor_tensor(t_scale[:], rstd[:], gam[:], ALU.mult).then_inc(t_chain, 1)
            dve.wait_ge(t_chain, i * CH + UNITS + 3)
            nc.vector.tensor_tensor(dev[:], t_scale[:], ps[:, STAT_BANK, 0:MT], ALU.mult).then_inc(t_chain, 1)
            dve.wait_ge(t_chain, i * CH + UNITS + 4)
            nc.vector.tensor_tensor(t_bias[:], bet[:], dev[:], ALU.subtract).then_inc(t_norm, 1)

        def finish(i, n):
            r = n % ACC_RING
            dve.wait_ge(prod_added, i * (NPT * N_GRAN) + NPT * (n + 1))
            dve.wait_ge(own, i * (OWN * N_GRAN) + OWN * (n + 1))
            nc.vector.tensor_tensor(acc_p[:, r, :], acc_p[:, r, :], acc_d[:, n % 2, :], ALU.add)\
                .then_inc(summed, 1)

        def granule(i, n, inserts, more, previous=True):
            u, q4 = n // GRANS, n % GRANS
            m0 = q4 * QM
            v = val[u % 2]

            def product(tap, dst):
                di, dj = tap // 3, tap % 3
                return nc.vector.tensor_tensor(
                    dst.rearrange("p (m r w) -> p m r w", m=QM, w=W),
                    taps_of(tap).rearrange("p (m r w) -> p m r w", m=1, w=W).to_broadcast([P, QM, UR, W]),
                    v[:, m0:m0 + QM, di:di + UR, dj:dj + W], ALU.mult)

            per = 1 if u == 0 else 2
            dve.wait_ge(kept, values_at(i, u, (m0 + QM) // per, more))
            if u > 0 and q4 == 0:
                dve.wait_ge(halo_ready, i * HALOS[3] + HALOS[u])
            g_own = i * (OWN * N_GRAN) + OWN * n
            j = d = 0
            for x, tap in enumerate(TAP_ORDER):
                b = bank_of[tap] - TAP0
                if q4 == 0 and half_of[tap] == 0:
                    dve.wait_ge(tap_ready, i * (UNITS * WV_BANKS) + WV_BANKS * u + b + 1)
                if tap in POOL_TAPS:
                    k = NPT * n + j
                    if not first(i, k - 1):
                        dve.wait_ge(prod_added, i * (NPT * N_GRAN) + k - 1)
                    product(tap, prod_p[:, k % 2, :]).then_inc(prod_ready, 1)
                    j += 1
                else:
                    product(tap, acc_d[:, n % 2, :] if d == 0 else prod_d[:, d - 1, :]).then_inc(own, 1)
                    d += 1
                if x == 1 and previous:
                    finish(i, n - 1)
                if x == 4:
                    dve.wait_ge(own, g_own + 2)
                    nc.vector.tensor_tensor(acc_d[:, n % 2, :], acc_d[:, n % 2, :], prod_d[:, 0, :], ALU.add)\
                        .then_inc(own, 1)
                if x == 7:
                    dve.wait_ge(own, g_own + 4)
                    nc.vector.tensor_tensor(acc_d[:, n % 2, :], acc_d[:, n % 2, :], prod_d[:, 1, :], ALU.add)\
                        .then_inc(own, 1)
                for at, work in inserts:
                    if at == x:
                        work()

        def period(i, more=True, begin=False):
            for n in range(N_GRAN):
                inserts = []
                if more:
                    if n in (3, 7, 11):
                        inserts.append((6, lambda u=n // 4: t_stats(i + 1, u)))
                    if n == 14:
                        inserts.append((1, lambda: (t_stats(i + 1, 3), t_aggregate(i + 1))))
                        inserts.append((7, lambda: t_spreads(i + 1)))
                    if n == 15:
                        inserts.append((1, lambda: t_add_eps(i + 1)))
                        inserts.append((6, lambda: t_affine(i + 1)))
                granule(i, n, inserts, more, previous=not (begin and n == 0))

        dve.wait_ge(const_in, 16 * 8)
        for m in range(MT):
            last = nc.vector.tensor_tensor(w2[:, m, :], w2[:, m, :], mask, ALU.mult)
        last.then_inc(w2_built, 1)
        dve.wait_ge(w2_built, 1)
        for u in range(UNITS):
            t_stats(0, u)
        t_aggregate(0)
        t_spreads(0)
        t_add_eps(0)
        t_affine(0)
        period(0, begin=True)
        with dve.Fori(1, B - 1) as i:
            period(i)
        period(B - 1, more=False)
        finish(B - 1, N_GRAN - 1)


PERMS = ((0, 1, 2, 3, 4, 5, 6, 7), (3, 0, 1, 2, 5, 6, 7, 4), (2, 3, 0, 1, 6, 7, 4, 5), (1, 2, 3, 0, 7, 4, 5, 6),
         (4, 5, 6, 7, 0, 1, 2, 3), (5, 6, 7, 4, 3, 0, 1, 2), (6, 7, 4, 5, 2, 3, 0, 1), (7, 4, 5, 6, 1, 2, 3, 0))


def kernel(x, L0_conv_kernel, L1_conv_w_v, L1_conv_w1, L1_conv_gn_gamma, L1_conv_gn_beta, L1_conv_w2, L1_conv_b2):
    import numpy as np
    import concourse.bacc as bacc
    from concourse.bass_utils import run_bass_kernel_spmd

    x = np.asarray(x)
    w_v, w1, w2, b2 = (np.asarray(a) for a in (L1_conv_w_v, L1_conv_w1, L1_conv_w2, L1_conv_b2))
    xl = np.ascontiguousarray(x.reshape(B, CG, STEPS, 2, 4, 2, H, W).transpose(0, 2, 5, 6, 3, 1, 4, 7)
                              ).reshape(B, STEPS, P, PAIRS * W)
    perms = np.array(PERMS)
    w1p = np.stack([w1[:, :, perms[g]] for g in range(GR)], axis=1)
    wvp = np.stack([w_v[:, :, perms[g]] for g in range(GR)], axis=1)

    def by_tile(a):
        n = a.shape[0]
        a = a.reshape(n, CG, KT, 4, GR)
        return np.ascontiguousarray(a.transpose(3, 1, 4, 2, 0)).reshape(P, KT, n)

    w1t = by_tile(w1p.reshape(CMID, 64, GR))
    wvt = by_tile(np.ascontiguousarray(wvp.reshape(CG, CM, GR, 64, GR).transpose(1, 0, 2, 3, 4)).reshape(C, 64, GR))
    a = np.arange(9).reshape(3, 3)
    turned = [a, np.rot90(a, 1), np.rot90(a, 2), np.rot90(a, 3), np.rot90(a.T, 3), np.rot90(a.T, 2),
              np.rot90(a.T, 1), a.T]
    turned = np.stack([m.reshape(9) for m in turned])
    w2k = w2.reshape(CG, 9, 32)[:, turned, :]
    w2k = w2k.transpose(3, 2, 0, 1).reshape(MT, 16, 1, 9 * 32)
    w2t = np.ascontiguousarray(np.broadcast_to(w2k, (MT, 16, GR, 9 * 32)).transpose(1, 2, 0, 3)).reshape(P, MT, 9 * 32)
    b2t = np.ascontiguousarray(np.broadcast_to(b2.reshape(1, CG, 9)[:, :, turned], (BANDS, CG, GR, 9))).reshape(P, 9)
    gam = np.ascontiguousarray(np.asarray(L1_conv_gn_gamma).reshape(MT, P).T)
    bet = np.ascontiguousarray(np.asarray(L1_conv_gn_beta).reshape(MT, P).T)
    kern = np.asarray(L0_conv_kernel).reshape(16)

    p = np.arange(P)
    shifts = np.zeros((P, TAPS0, P), np.float32)
    for u in range(TAPS0):
        shifts[:, u, :] = (p[:, None] // H == p[None, :] // H) & (p[:, None] % H == p[None, :] % H + u - 2)
    mean_a = np.full((P, P), 1.0 / P, np.float32)
    mean_b = ((p[:, None] // 8 == p[None, :] // 8) / 8.0).astype(np.float32)
    e = np.arange(8)
    member_of = ((e[None, :] // CG == p[:, None] // 64) & (e[None, :] % CG == p[:, None] // 8 % CG)).astype(np.float32)
    w2mask = np.ascontiguousarray(np.broadcast_to(
        (p[:, None, None] % 8 == np.arange(32)[None, None, :] % 8), (P, 9, 32)).astype(np.float32)).reshape(P, 288)

    arrays = dict(x=xl, shifts=shifts, mean_a=mean_a, kern=kern, member_of=member_of, w1t=w1t, wvt=wvt, w2t=w2t,
                  w2mask=w2mask, b2t=b2t, gamma=gam, beta=bet, mean_b=mean_b)
    nc = bacc.Bacc("TRN2", target_bir_lowering=False, num_devices=1)
    aps = {n: nc.dram_tensor(n, v.shape, F32, kind="ExternalInput").ap() for n, v in arrays.items()}
    out = nc.dram_tensor("out", (B, UNITS * GRANS, P, QM * UPX), F32, kind="ExternalOutput").ap()
    x1 = nc.dram_tensor("x1", (B, C, H, W), F32, kind="Internal").ap()
    program(nc, out=out, x1=x1, **aps)
    got = run_bass_kernel_spmd(nc, [arrays], core_ids=[0]).results[0]["out"]
    got = got.reshape(B, UNITS, GRANS, BANDS, CG, GR, QM, UR, W)
    return np.ascontiguousarray(got.transpose(0, 4, 2, 6, 5, 3, 1, 7, 8)).reshape(B, C, H, W)
```

```python
from contextlib import ExitStack

import concourse.bass as bass
from concourse import mybir

F32, F16, I32 = mybir.dt.float32, mybir.dt.float16, mybir.dt.int32
ALU = mybir.AluOpType
ACT = mybir.ActivationFunctionType
AX_X = mybir.AxisListType.X

P = 128
B, C, H, W = 16, 512, 64, 64
HW = H * W
CG, CM, GR = 4, 16, 8
EPS = 1e-5

STEPS = CM // 2
GPS = CG
PAIRS = 2 * CG * GR // 2
TAPS0 = 4
XP = 68
X_RING, OUT_RING = 8, 4
N_RING, U_RING = 4, 2
BUILT = 7 + TAPS0 + 2

UP = 64.0
EXPONENT = 0x7F800000
TINY = 2.0 ** -100

BANDS = 4
UNITS, UR = 4, 4
UPX = UR * W
KT = C // P
CMID = 32 * GR
MT = CMID // P
TAPS1 = 9
QM = 4
GRANS = CM // QM
VP = W + 2
BR = H // BANDS + 2
ROWS = [6, 4, 4, 4]
AHEAD = GRANS - 1
P_TAPS, D_TAPS = (0, 2, 4, 5, 7, 8), (1, 3, 6)
NP = len(P_TAPS)
ADD_AT = (4, 7)
FINISH_AT = 3
WV_BANKS = 5
ACC_RING = 4
LOAD_AT = {1: 0, 5: 1, 9: 2}
LOAD_LAST_AT = 15
NORMALIZE_AT = {2: 0, 6: 1, 10: 2}
ABOVE_AT = 9
RSTD_AT = (14, 4)
WHOLE = 2
SETUP = 4


def wait_apart(engine, apart, sem, value):
    engine.wait_ge(sem, value)
    engine.sem_inc(apart, 1)


def program(nc, x, shifts, mean_a, kern, member_of, w1t, wvt, w2t, w2mask, b2t, gamma, beta, mean_b, out, x1):
    with ExitStack() as top:
        def sem(name, ctx=top):
            return ctx.enter_context(nc.semaphore(name))

        ps = top.enter_context(nc.psum_tensor("ps", [P, 8, 512], F32))
        x1_scale = top.enter_context(nc.sbuf_tensor("x1_scale", [P, B * KT], F32))
        x1_bias = top.enter_context(nc.sbuf_tensor("x1_bias", [P, B * KT], F32))
        with ExitStack() as ctx:
            stage_a(nc, ctx, sem, ps, x, shifts, mean_a, kern, member_of, x1, x1_scale, x1_bias)
        with ExitStack() as ctx:
            stage_b(nc, ctx, sem, ps, x1, w1t, wvt, w2t, w2mask, b2t, gamma, beta, mean_b, out, x1_scale, x1_bias)


def stage_a(nc, ctx, sem, ps, x, shifts, mean_a, kern, member_of, x1, x1_scale, x1_bias):
    def sb(name, shape, dtype=F32):
        return ctx.enter_context(nc.sbuf_tensor(name, shape, dtype))

    NS = B * STEPS
    x_in = sb("x_in", [P, X_RING, PAIRS * W])
    x_out = sb("x_out", [P, OUT_RING, PAIRS * W])
    xn = sb("xn", [P, U_RING, PAIRS * W])
    xn_hi = sb("xn_hi", [P, N_RING, PAIRS * XP], F16)
    xn_lo = sb("xn_lo", [P, N_RING, PAIRS * XP], F16)
    shift_m = sb("shift_m", [P, TAPS0, P])
    band = sb("band", [P, TAPS0, P])
    band_hi = sb("band_hi", [P, TAPS0, P], F16)
    band_lo = sb("band_lo", [P, TAPS0, P], F16)
    kern_b = sb("kern_b", [P, TAPS0 * TAPS0])
    kern_abs = sb("kern_abs", [P, TAPS0 * TAPS0])
    kern_max = sb("kern_max", [P, 1])
    kern_one = sb("kern_one", [P, 1])
    unscale = sb("unscale", [P, 1])
    ones = sb("ones", [P, P])
    member = sb("member", [P, 2 * CG])
    power = sb("power", [P, GPS])
    table_s = sb("table_s", [P, B, STEPS * GPS])
    table_b = sb("table_b", [P, B, STEPS * GPS])
    pick = sb("pick", [P, B * KT, 2 * CG])
    six = sb("six", [P, 2 * GPS, 6])
    mv = sb("mv", [P, 2 * GPS, 2])
    dev = sb("dev", [P, 2 * GPS])
    spread = sb("spread", [P, 2 * GPS])
    var_eps = sb("var_eps", [P, 2 * GPS])
    norm_s = sb("norm_s", [P, 2, GPS])
    norm_b = sb("norm_b", [P, 2, GPS])

    const_in = sem("a_const_in")
    sp_apart, dve_apart = sem("a_sp_apart"), sem("a_dve_apart")
    setup = sem("a_setup")
    built = sem("built")
    x_loaded = [sem(f"x_loaded{r}") for r in range(X_RING)]
    x1_stored = [sem(f"x1_stored{r}") for r in range(OUT_RING)]
    x_added = sem("x_added")
    hi_ready = sem("hi_ready")
    lo_ready = sem("lo_ready")
    blurred = sem("blurred")
    norm_ready = sem("norm_ready")
    local_done = sem("local_done")
    mean_done = sem("mean_done")
    spread_done = sem("spread_done")
    var_done = sem("var_done")
    var_eps_done = sem("var_eps_done")
    rstd_done = sem("rstd_done")
    rstd1_done = sem("rstd1_done")
    stats_chain = sem("stats_chain")
    table_done = sem("table_done")
    picked = sem("picked")

    MEAN_BANK, VAR_BANK = 4, 5
    BLUR_LAG, X1_LAG = 3, 4
    FIRST = BLUR_LAG + OUT_RING
    LAST = STEPS + X1_LAG + 1

    def has(i, k, lag=0):
        return not isinstance(i, int) or 0 <= i * STEPS + k - lag < NS

    def group(buf, pitch, width, lo, g):
        return buf.rearrange("p (m c h w) -> p m c h w", m=2, c=CG, w=pitch)[:, :, g, :, lo:lo + width]

    def where(i, k):
        return i + k // STEPS, k % STEPS

    def columns(i, k):
        return slice(0 if has(i, k) else GPS, 2 * GPS if has(i, k, X1_LAG) else GPS)

    def pipeline(engine, slot):
        for k in range(FIRST):
            slot(0, k)
        with engine.Fori(0, B - 1) as i:
            for k in range(FIRST, FIRST + STEPS):
                slot(i, k)
        for k in range(FIRST, LAST + 1):
            slot(B - 1, k)

    block = ctx.enter_context(nc.Block())

    @block.sync
    def _(sp):
        def load(i, k):
            img, s = where(i, k)
            sp.dma_start(x_in[:, k % X_RING, :], x[img, s]).then_inc(x_loaded[k % X_RING], 16)

        def store(i, k):
            img, s = where(i, k)
            src = x_out[:, k % OUT_RING, :].rearrange("p (m a w) -> p m a w", m=2, w=W)
            for m in range(2):
                dst = x1[img, (2 * s + m) * 32:(2 * s + m + 1) * 32].rearrange("(a t) h w -> (t h) a w", t=2)
                sp.dma_start(dst, src[:, m]).then_inc(x1_stored[k % OUT_RING], 16)

        def slot(i, k, more=True):
            wait_apart(sp, sp_apart, x_added, i * (STEPS * GPS) + GPS * (k + 1))
            store(i, k)
            if more:
                load(i, k + X_RING)

        load(0, 0)
        for dst, src in ((ones, mean_a), (kern_b, kern.partition_broadcast(P)), (shift_m, shifts),
                         (member, member_of)):
            sp.dma_start(dst[:], src).then_inc(const_in, 16)
        for k in range(1, X_RING):
            load(0, k)
        with sp.Fori(0, B - 1) as i:
            for k in range(STEPS):
                slot(i, k)
        for k in range(STEPS):
            slot(B - 1, k, more=False)
        for r in range(OUT_RING):
            sp.wait_ge(x1_stored[r], 32 * (NS // OUT_RING))

    @block.scalar
    def _(act):
        def normalize(i, k):
            r = k % N_RING
            act.wait_ge(norm_ready, i * STEPS + k + 1)
            if has(i, k, 2):
                act.wait_ge(lo_ready, i * (STEPS * GPS) + GPS * (k - 1))
            if has(i, k, N_RING):
                act.wait_ge(blurred, i * (STEPS * GPS) + GPS * (k - N_RING + 1))
            for g in range(GPS):
                src = group(x_in[:, k % X_RING, :], W, W, 0, g)
                for dst in (group(xn_hi[:, r, :], XP, W, 2, g), group(xn[:, k % U_RING, :], W, W, 0, g)):
                    nc.scalar.activation(dst, src, ACT.Identity, bias=norm_b[:, k % 2, g:g + 1],
                                         scale=norm_s[:, k % 2, g:g + 1]).then_inc(hi_ready, 1)

        act.wait_ge(setup, 5)
        for k in range(N_RING):
            normalize(0, k)
        with act.Fori(0, B - 1) as i:
            for k in range(N_RING, N_RING + STEPS):
                normalize(i, k)
        for k in range(N_RING, STEPS):
            normalize(B - 1, k)

    @block.tensor
    def _(pe):
        def mean_over_partitions(i, k):
            c = columns(i, k)
            pe.wait_ge(local_done, i * STEPS + k + 1)
            nc.tensor.matmul(ps[:, MEAN_BANK, c], ones[:], mv[:, c, 0], start=True, stop=True)\
                .then_inc(mean_done, 1)

        def var_over_partitions(i, k):
            c = columns(i, k)
            pe.wait_ge(spread_done, i * STEPS + k + 1)
            nc.tensor.matmul(ps[:, VAR_BANK, c], ones[:], spread[:, c], start=True, stop=True)\
                .then_inc(var_done, 1)

        def blur(i, k, g):
            n = i * (STEPS * GPS) + GPS * k + g
            pe.wait_ge(lo_ready, n + 1)
            if has(i, k, 1):
                pe.wait_ge(x_added, n - GPS + 1)
            parts = [(band_hi, xn_hi), (band_hi, xn_lo), (band_lo, xn_hi)]
            for v in range(TAPS0):
                for j, (weights, data) in enumerate(parts):
                    mm = nc.tensor.matmul(ps[:, g, :], weights[:, v, :], group(data[:, k % N_RING, :], XP, W, v, g),
                                          start=(v == 0 and j == 0), stop=(v == TAPS0 - 1 and j == 2))
            mm.then_inc(blurred, 1)

        def slot(i, k):
            blurs = has(i, k, BLUR_LAG)
            if blurs:
                blur(i, k - BLUR_LAG, 0)
            if k >= 1 and (has(i, k, 1) or has(i, k, X1_LAG + 1)):
                var_over_partitions(i, k - 1)
            if blurs:
                blur(i, k - BLUR_LAG, 1)
                blur(i, k - BLUR_LAG, 2)
                blur(i, k - BLUR_LAG, 3)
            if has(i, k) or has(i, k, X1_LAG):
                mean_over_partitions(i, k)

        pe.wait_ge(const_in, 64)
        pe.wait_ge(built, BUILT)
        pipeline(pe, slot)

    @block.gpsimd
    def _(pool):
        nc.gpsimd.memset(power[:], -0.5).then_inc(setup, 1)
        for buf in (xn_hi, xn_lo):
            rows = buf[:].rearrange("p r (a w) -> p (r a) w", w=XP)
            nc.gpsimd.memset(rows[:, :, 0:2], 0.0).then_inc(setup, 1)
            nc.gpsimd.memset(rows[:, :, 2 + W:], 0.0).then_inc(setup, 1)
        pool.wait_ge(setup, 5)

        def slot(i, k):
            if has(i, k, 1) or has(i, k, X1_LAG + 1):
                pool.wait_ge(var_eps_done, i * STEPS + k)
            if has(i, k, 1):
                nc.gpsimd.tensor_tensor(norm_s[:, (k - 1) % 2, :], var_eps[:, 0:GPS], power[:], ALU.pow)\
                    .then_inc(rstd_done, 1)
            if has(i, k, X1_LAG + 1):
                img, s = where(i, k - X1_LAG - 1)
                nc.gpsimd.tensor_tensor(table_s[:, img, s * GPS:(s + 1) * GPS], var_eps[:, GPS:], power[:], ALU.pow)\
                    .then_inc(rstd1_done, 1)
            if has(i, k, 1):
                for g in range(GPS):
                    r = (k - 1) % N_RING
                    pool.wait_ge(hi_ready, i * (2 * STEPS * GPS) + 2 * GPS * (k - 1) + 2 * g + 2)
                    nc.gpsimd.tensor_tensor(group(xn_lo[:, r, :], XP, W, 2, g),
                                            group(xn[:, (k - 1) % U_RING, :], W, W, 0, g),
                                            group(xn_hi[:, r, :], XP, W, 2, g), ALU.subtract).then_inc(lo_ready, 1)

        pipeline(pool, slot)

    @block.vector
    def _(dve):
        CHAIN = 3

        def chain_at(i, k, n):
            return i * (STEPS * CHAIN) + CHAIN * k + n

        def local_stats(buf, j):
            for g in range(GPS):
                last = nc.vector.bn_stats(six[:, j * GPS + g, :],
                                          buf.rearrange("p (m c w) -> p m c w", m=2, c=CG)[:, :, g, :])
            return last

        def aggregate(i, k):
            c = columns(i, k)
            wait_apart(dve, dve_apart, stats_chain, chain_at(i, k, 1))
            for g in range(c.start, c.stop):
                last = nc.vector.bn_aggr(mv[:, g, :], six[:, g, :])
            last.then_inc(local_done, 1)

        def spreads(i, k):
            c = columns(i, k)
            dve.wait_ge(local_done, i * STEPS + k + 1)
            dve.wait_ge(mean_done, i * STEPS + k + 1)
            nc.vector.tensor_tensor(dev[:, c], mv[:, c, 0], ps[:, MEAN_BANK, c], ALU.subtract)\
                .then_inc(stats_chain, 1)
            dve.wait_ge(stats_chain, chain_at(i, k, 2))
            nc.vector.tensor_tensor(dev[:, c], dev[:, c], dev[:, c], ALU.mult).then_inc(stats_chain, 1)
            dve.wait_ge(stats_chain, chain_at(i, k, 3))
            nc.vector.tensor_tensor(spread[:, c], dev[:, c], mv[:, c, 1], ALU.add).then_inc(spread_done, 1)

        def add_eps(i, k):
            c = columns(i, k)
            dve.wait_ge(var_done, i * STEPS + k + 1)
            nc.vector.tensor_scalar(var_eps[:, c], ps[:, VAR_BANK, c], EPS, UP ** -2, ALU.add, ALU.mult)\
                .then_inc(var_eps_done, 1)

        def offset(mean, rstd, dst, done):
            nc.vector.scalar_tensor_tensor(out=dst, in0=mean, scalar=-1.0, in1=rstd,
                                           op0=ALU.mult, op1=ALU.mult).then_inc(done, 1)

        def offsets(i, k):
            if has(i, k):
                dve.wait_ge(rstd_done, i * STEPS + k + 1)
                offset(ps[:, MEAN_BANK, 0:GPS], norm_s[:, k % 2, :], norm_b[:, k % 2, :], norm_ready)
            if has(i, k, X1_LAG):
                img, s = where(i, k - X1_LAG)
                dve.wait_ge(rstd1_done, i * STEPS + k - X1_LAG + 1)
                offset(ps[:, MEAN_BANK, GPS:2 * GPS], table_s[:, img, s * GPS:(s + 1) * GPS],
                       table_b[:, img, s * GPS:(s + 1) * GPS], table_done)

        def add_x(i, k, g):
            r = k % OUT_RING
            dve.wait_ge(blurred, i * (STEPS * GPS) + GPS * k + g + 1)
            if g == 0 and has(i, k, OUT_RING):
                dve.wait_ge(x1_stored[r], i * (32 * STEPS // OUT_RING) + 32 * (k // OUT_RING))
            nc.vector.scalar_tensor_tensor(out=group(x_out[:, r, :], W, W, 0, g).rearrange("p m h w -> p m (h w)"),
                                           in0=ps[:, g, :].rearrange("p (m n) -> p m n", m=2),
                                           scalar=unscale[:, 0:1],
                                           in1=group(x_in[:, k % X_RING, :], W, W, 0, g)
                                           .rearrange("p m h w -> p m (h w)"),
                                           op0=ALU.mult, op1=ALU.add).then_inc(x_added, 1)

        def slot(i, k):
            now, now1 = has(i, k), has(i, k, X1_LAG)
            before = k >= 1 and (has(i, k, 1) or has(i, k, X1_LAG + 1))
            adds = has(i, k, BLUR_LAG)
            last = None
            if before:
                spreads(i, k - 1)
            if now:
                dve.wait_ge(x_loaded[k % X_RING], i * (16 * STEPS // X_RING) + 16 * (k // X_RING + 1))
                last = local_stats(x_in[:, k % X_RING, :], 0)
            if adds:
                add_x(i, k - BLUR_LAG, 0)
            if before:
                add_eps(i, k - 1)
            if now1:
                dve.wait_ge(x_added, i * (STEPS * GPS) + GPS * (k - X1_LAG + 1))
                last = local_stats(x_out[:, (k - X1_LAG) % OUT_RING, :], 1)
            if last is not None:
                last.then_inc(stats_chain, 1)
            if adds:
                add_x(i, k - BLUR_LAG, 1)
            if before:
                offsets(i, k - 1)
            if now or now1:
                aggregate(i, k)
            if adds:
                add_x(i, k - BLUR_LAG, 2)
                add_x(i, k - BLUR_LAG, 3)

        dve.wait_ge(const_in, 64)
        nc.vector.scalar_tensor_tensor(out=kern_abs[:], in0=kern_b[:], scalar=-1.0, in1=kern_b[:],
                                       op0=ALU.mult, op1=ALU.max).then_inc(built, 1)
        dve.wait_ge(built, 1)
        nc.vector.tensor_reduce(kern_max[:], kern_abs[:], AX_X, ALU.max).then_inc(built, 1)
        dve.wait_ge(built, 2)
        nc.vector.tensor_scalar(kern_max[:], kern_max[:], TINY, None, ALU.max).then_inc(built, 1)
        dve.wait_ge(built, 3)
        nc.vector.tensor_scalar(kern_one[:].bitcast(I32), kern_max[:].bitcast(I32), EXPONENT, None, ALU.bitwise_and)\
            .then_inc(built, 1)
        dve.wait_ge(built, 4)
        nc.vector.tensor_scalar(unscale[:], kern_one[:], 1 / UP, None, ALU.mult).then_inc(built, 1)
        nc.vector.reciprocal(kern_max[:], kern_one[:]).then_inc(built, 1)
        dve.wait_ge(built, 6)
        nc.vector.tensor_scalar(kern_b[:], kern_b[:], kern_max[:, 0:1], None, ALU.mult).then_inc(built, 1)
        n = 7
        dve.wait_ge(built, n)
        for u in range(TAPS0):
            for v in range(TAPS0):
                j = (TAPS0 - 1 - u) * TAPS0 + TAPS0 - 1 - v
                if u == 0:
                    last = nc.vector.tensor_scalar(band[:, v, :], shift_m[:, u, :], kern_b[:, j:j + 1], None, ALU.mult)
                else:
                    last = nc.vector.scalar_tensor_tensor(out=band[:, v, :], in0=shift_m[:, u, :],
                                                          scalar=kern_b[:, j:j + 1], in1=band[:, v, :],
                                                          op0=ALU.mult, op1=ALU.add)
            last.then_inc(built, 1)
            n += 1
            dve.wait_ge(built, n)
        nc.vector.tensor_copy(band_hi[:], band[:]).then_inc(built, 1)
        dve.wait_ge(built, n + 1)
        nc.vector.tensor_tensor(band_lo[:], band[:], band_hi[:], ALU.subtract).then_inc(built, 1)
        pipeline(dve, slot)
        dve.wait_ge(table_done, NS)
        n = 0
        for table, dst in ((table_s, x1_scale), (table_b, x1_bias)):
            nc.vector.scalar_tensor_tensor(out=pick[:], in0=table[:].rearrange("p b (t e) -> p (b t) e", e=2 * CG),
                                           scalar=1 / UP, in1=member[:].unsqueeze(1).to_broadcast([P, B * KT, 2 * CG]),
                                           op0=ALU.mult, op1=ALU.mult)\
                .then_inc(picked, 1)
            n += 1
            dve.wait_ge(picked, n)
            nc.vector.tensor_reduce(dst[:], pick[:], AX_X, ALU.add).then_inc(picked, 1)
            n += 1
            dve.wait_ge(picked, n)


def stage_b(nc, ctx, sem, ps, x1, w1t, wvt, w2t, w2mask, b2t, gamma, beta, mean_b, out, x1_scale, x1_bias):
    def sb(name, shape, dtype=F32):
        return ctx.enter_context(nc.sbuf_tensor(name, shape, dtype))

    xm = sb("xm", [P, KT, BANDS * BR * W])
    xs = sb("xs", [P, KT, BANDS * UPX])
    t = sb("t", [P, MT, UNITS, BANDS * UPX])
    t_last = sb("t_last", [P, MT, BANDS * UPX])
    val = sb("val", [P, CM, UR + 2, VP])
    acc = sb("acc", [P, ACC_RING, QM * UPX])
    acc_d = sb("acc_d", [P, 2, QM * UPX])
    prod_p = sb("prod_p", [P, 2, QM * UPX])
    prod_d = sb("prod_d", [P, QM * UPX])
    w1 = sb("w1", [P, KT, CMID])
    wv = sb("wv", [P, KT, CM * 32])
    w2 = sb("w2", [P, MT, TAPS1 * 32])
    blk = sb("blk", [P, P])
    b2 = sb("b2", [P, TAPS1])
    gam = sb("gam", [P, MT])
    bet = sb("bet", [P, MT])
    power = sb("power_b", [P, MT])
    six = sb("six_t", [P, MT, 2 * UNITS, 6])
    mv = sb("mv_t", [P, MT, 2])
    dev = sb("dev_t", [P, MT])
    spread = sb("spread_t", [P, MT])
    var_eps = sb("var_eps_t", [P, MT])
    rstd = sb("rstd_t", [P, MT])
    t_scale = sb("t_scale", [P, MT])
    t_bias = sb("t_bias", [P, MT])
    mask = prod_d[:, 0:TAPS1 * 32]

    w1_in, const_in = sem("w1_in"), sem("b_const_in")
    sp_apart, act_apart, dve_apart = (sem(f"b_{e}_apart") for e in ("sp", "act", "dve"))
    setup = sem("b_setup")
    w2_built = sem("w2_built")
    xm_loaded = [sem(f"xm_loaded{u}") for u in range(UNITS)]
    xm_ready = sem("xm_ready")
    xs_ready = sem("xs_ready")
    xm_above = sem("xm_above")
    xm_whole = sem("xm_whole")
    mm_full = sem("mm_full")
    kept = sem("kept")
    halo_ready = sem("halo_ready")
    t_ready = sem("t_ready")
    tap_mm = sem("tap_mm")
    tap_ready = sem("tap_ready")
    p_ready = sem("p_ready")
    p_added = sem("p_added")
    own = sem("own")
    summed = sem("summed")
    resid_in = [sem(f"resid_in{r}") for r in range(ACC_RING)]
    stored = [sem(f"stored{r}") for r in range(ACC_RING)]
    t_chain = sem("t_chain")
    t_local, t_mean, t_spread, t_var, t_var_eps, t_rstd, t_norm = (
        sem(n) for n in ("t_local", "t_mean", "t_spread", "t_var", "t_var_eps", "t_rstd", "t_norm"))

    RING0, STAT_BANK = WV_BANKS, 7
    N_GRAN = UNITS * GRANS
    banks = [range(TAPS1)[2 * b:2 * b + 2] for b in range(WV_BANKS)]
    V_BANKS = [QM if n < GRANS else QM // 2 for n in range(N_GRAN)]
    OWN = 5
    LEAD_MM = 4 * UNITS + sum(V_BANKS[:AHEAD])
    PERIOD_MM = 4 * UNITS + sum(V_BANKS)
    CONV_AT = {1: (3, 0), 2: (0, 0), 4: (0, 1), 5: (3, 1), 6: (1, 0), 8: (1, 1), 10: (2, 0), 11: (2, 1)}

    def taps_of(tap):
        return ps[:, tap // 2, tap % 2 * UPX:(tap % 2 + 1) * UPX]

    def period_base(i):
        return i * PERIOD_MM + LEAD_MM

    def values_end(i, n, more=True):
        if n < AHEAD:
            return period_base(i) - sum(V_BANKS[n + 1:AHEAD])
        return period_base(i) + sum(V_BANKS[AHEAD:n + 1]) + \
            (2 * sum(s < n - AHEAD for s in CONV_AT) if more else 0)

    def t_end(i, u):
        if isinstance(i, int) and i == 0:
            return 4 * (u + 1)
        last = max(step for step, (unit, _) in CONV_AT.items() if unit == u)
        return period_base(i) - PERIOD_MM + sum(V_BANKS[AHEAD:last + AHEAD + 1]) + 2 * sum(x <= last for x in CONV_AT)

    def product_done(i, n, tap):
        if tap in P_TAPS:
            return p_ready, i * (NP * N_GRAN) + NP * n + P_TAPS.index(tap) + 1
        return own, i * (OWN * N_GRAN) + OWN * n + (1, 2, 4)[D_TAPS.index(tap)]

    def granule_done(i, n):
        return product_done(i, n, TAPS1 - 1)

    def halo_count(i, n):
        return i * (N_GRAN - GRANS) + max(n - GRANS + 1, 0)

    def first(i, k=0):
        return isinstance(i, int) and i == 0 and k <= 0

    def xm_rows(kt, u):
        return xm[:, kt, :].rearrange("p (q n) -> p q n", q=BANDS)[:, :, W + u * UPX:W + (u + 1) * UPX]

    def xs_rows(kt):
        return xs[:, kt, :].rearrange("p (q n) -> p q n", q=BANDS)

    block = ctx.enter_context(nc.Block())

    @block.sync
    def _(sp):
        def load_xm(i, u):
            if u == UNITS - 1:
                if not first(i):
                    wait_apart(sp, sp_apart, xm_whole, WHOLE * i)
            elif not first(i):
                wait_apart(sp, sp_apart, mm_full, values_end(i - 1, GRANS * u + GRANS - 1))
            for kt in range(KT):
                src = x1[i, kt * P:(kt + 1) * P].rearrange("c (q r) w -> c q (r w)", q=BANDS)[
                    :, :, u * UPX:(u + 1) * UPX]
                sp.dma_start(xs_rows(kt) if u == UNITS - 1 else xm_rows(kt, u), src).then_inc(xm_loaded[u], 16)

        def load_resid(i, n):
            u, q4, r = (n // GRANS) % UNITS, n % GRANS, n % ACC_RING
            if not first(i, n - ACC_RING + 1):
                wait_apart(sp, sp_apart, stored[r], i * (16 * N_GRAN // ACC_RING) + 16 * (n // ACC_RING))
            img = i + n // N_GRAN
            for q in range(BANDS):
                src = x1[img].rearrange("(m e) h w -> e m (h w)", m=CM)[
                    :, q4 * QM:(q4 + 1) * QM, (q * 16 + u * UR) * W:(q * 16 + (u + 1) * UR) * W]
                dst = acc[32 * q:32 * q + 32, r, :].rearrange("p (m n) -> p m n", m=QM)
                sp.dma_start(dst, src).then_inc(resid_in[r], 16)

        def store(i, n):
            wait_apart(sp, sp_apart, summed, i * N_GRAN + n + 1)
            img, m = (i + n // N_GRAN, n % N_GRAN) if n >= 0 else (i - 1, n + N_GRAN)
            sp.dma_start(out[img, m], acc[:, n % ACC_RING, :]).then_inc(stored[n % ACC_RING], 16)

        load_xm(0, 0)
        sp.dma_start(w1[:], w1t).then_inc(w1_in, 16)
        load_xm(0, 1)
        for dst, src in ((w2, w2t), (wv, wvt), (blk, mean_b), (b2, b2t), (gam, gamma), (bet, beta)):
            sp.dma_start(dst[:], src).then_inc(const_in, 16)
        sp.dma_start(mask, w2mask).then_inc(const_in, 16)
        load_xm(0, 2)
        load_xm(0, 3)
        load_resid(0, 0)
        load_resid(0, 1)
        load_xm(1, UNITS - 1)

        def period(i, more=True, ahead=True, begin=False):
            for n in range(N_GRAN):
                if more and n in LOAD_AT:
                    load_xm(i + 1, LOAD_AT[n])
                if ahead and n == LOAD_LAST_AT:
                    load_xm(i + 2, UNITS - 1)
                if more or n + 2 < N_GRAN:
                    load_resid(i, n + 2)
                if not (begin and n == 0):
                    store(i, n - 1)

        period(0, begin=True)
        with sp.Fori(1, B - 2) as i:
            period(i)
        period(B - 2, ahead=False)
        period(B - 1, more=False, ahead=False)
        store(B - 1, N_GRAN - 1)
        for r in range(ACC_RING):
            sp.wait_ge(stored[r], 16 * B * N_GRAN // ACC_RING)

    @block.tensor
    def _(pe):
        class Ring:
            base, n = 0, 0

        def take():
            if not (isinstance(Ring.base, int) and Ring.base == 0 and Ring.n < 2):
                pe.wait_ge(kept, Ring.base + Ring.n - 1)
            b = RING0 + Ring.n % 2
            Ring.n += 1
            return b

        def conv_t(i, u, halves):
            if u == UNITS - 1:
                pe.wait_ge(xs_ready, KT * (i + 1))
            else:
                pe.wait_ge(xm_ready, i * (KT * (UNITS - 1)) + KT * (u + 1))
            for m in halves:
                for h in range(2):
                    b = take()
                    for kt in range(KT):
                        rows = xs_rows(kt) if u == UNITS - 1 else xm_rows(kt, u)
                        mm = nc.tensor.matmul(ps[:, b, :], w1[:, kt, m * P:(m + 1) * P],
                                              rows[:, 2 * h:2 * h + 2, :], start=(kt == 0), stop=(kt == KT - 1))
                    mm.then_inc(mm_full, 1)

        def values(n, halves=(0, 1)):
            u, m0 = n // GRANS, n % GRANS * QM
            per = QM // V_BANKS[n]
            for m in range(m0 + halves[0] * QM // 2, m0 + (halves[-1] + 1) * QM // 2, per):
                b = take()
                for x in range(per):
                    row, at = (0 if u == 0 else u * UR + 2), x * ROWS[u] * W
                    for kt in range(KT):
                        for q in range(BANDS):
                            r0 = (q * BR + row) * W
                            mm = nc.tensor.matmul(ps[32 * q:32 * q + 32, b, at:at + ROWS[u] * W],
                                                  wv[:, kt, (m + x) * 32:(m + x + 1) * 32],
                                                  xm[:, kt, r0:r0 + ROWS[u] * W],
                                                  start=(kt == 0), stop=(kt == KT - 1), skip_group_check=True)
                mm.then_inc(mm_full, 1)

        def tap_weights(i, u):
            pe.wait_ge(t_ready, i * (MT * UNITS) + MT * (u + 1))
            for b in range(WV_BANKS):
                if not first(i, u):
                    pe.wait_ge(*product_done(i, GRANS * u - 1, banks[b][-1]))
                for tap in banks[b]:
                    for kt in range(MT):
                        for q in range(BANDS):
                            mm = nc.tensor.matmul(taps_of(tap)[32 * q:32 * q + 32, :],
                                                  w2[:, kt, tap * 32:(tap + 1) * 32],
                                                  t[:, kt, u, q * UPX:(q + 1) * UPX],
                                                  start=(kt == 0), stop=(kt == MT - 1),
                                                  skip_group_check=True)
                mm.then_inc(tap_mm, 1)

        def means(i):
            pe.wait_ge(t_local, i + 1)
            nc.tensor.matmul(ps[:, STAT_BANK, 0:MT], blk[:], mv[:, :, 0], start=True, stop=True).then_inc(t_mean, 1)

        def variances(i):
            pe.wait_ge(t_spread, i + 1)
            nc.tensor.matmul(ps[:, STAT_BANK, 8:8 + MT], blk[:], spread[:], start=True, stop=True)                .then_inc(t_var, 1)

        def lead(i):
            pe.wait_ge(xm_above, i + 1)
            values(0)
            means(i)
            values(1, [0])
            variances(i)
            values(1, [1])
            values(2, [0])
            tap_weights(i, 0)
            values(2, [1])

        pe.wait_ge(w1_in, 16)
        for u in range(UNITS):
            conv_t(0, u, range(MT))
        pe.wait_ge(const_in, 16 * 7)
        pe.wait_ge(setup, SETUP)
        pe.wait_ge(w2_built, 1)
        pe.wait_ge(xm_above, 1)
        values(0)
        means(0)
        variances(0)
        tap_weights(0, 0)
        values(1)
        values(2)

        def period(i, more=True):
            Ring.base, Ring.n = i * PERIOD_MM, LEAD_MM
            for n in range(N_GRAN):
                if n % GRANS == GRANS - 1 and n < N_GRAN - 1:
                    tap_weights(i, n // GRANS + 1)
                if n + AHEAD == 2 * GRANS:
                    pe.wait_ge(xm_whole, WHOLE * (i + 1))
                if n + AHEAD < N_GRAN:
                    values(n + AHEAD)
                if more and n in CONV_AT:
                    u, half = CONV_AT[n]
                    conv_t(i + 1, u, [half])
            if more:
                lead(i + 1)

        period(0)
        with pe.Fori(1, B - 1) as i:
            period(i)
        period(B - 1, more=False)

    @block.scalar
    def _(act):
        class Ring:
            base, n = 0, 0

        def take():
            act.wait_ge(mm_full, Ring.base + Ring.n + 1)
            b = RING0 + Ring.n % 2
            Ring.n += 1
            return b

        def normalize(i, u):
            wait_apart(act, act_apart, xm_loaded[u], (i + 1) * (16 * KT))
            for kt in range(KT):
                v, done = (xs_rows(kt), xs_ready) if u == UNITS - 1 else (xm_rows(kt, u), xm_ready)
                nc.scalar.activation(v, v, ACT.Identity, bias=x1_bias[:, bass.ds(i * KT + kt, 1)],
                                     scale=x1_scale[:, bass.ds(i * KT + kt, 1)]).then_inc(done, 1)

        bands = xm[:].rearrange("p k (q n) -> p k q n", q=BANDS)
        last_rows = xs[:].rearrange("p k (q n) -> p k q n", q=BANDS)

        def rows_above(i):
            if not first(i):
                act.wait_ge(mm_full, values_end(i - 1, GRANS - 1))
            act.wait_ge(xs_ready, KT * (i + 1))
            nc.scalar.activation(bands[:, :, 1:, 0:W], last_rows[:, :, 0:BANDS - 1, UPX - W:], ACT.Copy)                .then_inc(xm_above, 1)

        def complete(i):
            if not first(i):
                act.wait_ge(mm_full, values_end(i - 1, N_GRAN - 1))
            act.wait_ge(xm_ready, (i + 1) * (KT * (UNITS - 1)))
            nc.scalar.activation(bands[:, :, 0:BANDS - 1, (BR - 1) * W:], bands[:, :, 1:, W:2 * W], ACT.Copy)                .then_inc(xm_whole, 1)
            lo = W + (UNITS - 1) * UPX
            nc.scalar.activation(bands[:, :, :, lo:lo + UPX], last_rows, ACT.Copy).then_inc(xm_whole, 1)

        def keep_t(i, u, halves):
            if u == UNITS - 1 and not first(i):
                act.wait_ge(t_ready, i * (MT * UNITS))
            for m in halves:
                for h in range(2):
                    b = take()
                    dst = (t_last[:, m, :] if u == UNITS - 1 else t[:, m, u, :])[:, 512 * h:512 * (h + 1)]
                    nc.scalar.activation(dst, ps[:, b, :], ACT.Copy).then_inc(kept, 1)

        def keep_values(i, n, halves=(0, 1)):
            u, m0 = n // GRANS, n % GRANS * QM
            per = QM // V_BANKS[n]
            img, before = (i, n - GRANS) if n >= GRANS else (i - 1, n - GRANS + N_GRAN)
            v = val[:, m0:m0 + QM]
            if not first(i, n - GRANS + 1):
                act.wait_ge(*granule_done(img, before))
            if u > 0:
                act.wait_ge(kept, values_end(i, n - GRANS, Ring.more))
                nc.scalar.activation(v[:, :, 0:2, 1:1 + W], v[:, :, 4:6, 1:1 + W], ACT.Copy).then_inc(halo_ready, 1)
            if not first(i, n - GRANS + 1):
                act.wait_ge(halo_ready, halo_count(i, n))
            for m in range(m0 + halves[0] * QM // 2, m0 + (halves[-1] + 1) * QM // 2, per):
                b = take()
                src = ps[:, b, 0:per * ROWS[u] * W].rearrange("p (m r w) -> p m r w", m=per, w=W)
                lo = 0 if u == 0 else 2
                nc.scalar.activation(val[:, m:m + per, lo:lo + ROWS[u], 1:1 + W], src, ACT.Copy)                    .then_inc(kept, 1)

        def tap_bias(i, u):
            for b in range(WV_BANKS):
                act.wait_ge(tap_mm, i * (UNITS * WV_BANKS) + WV_BANKS * u + b + 1)
                for tap in banks[b]:
                    last = nc.scalar.activation(taps_of(tap), taps_of(tap), ACT.Identity, bias=b2[:, tap:tap + 1])
                last.then_inc(tap_ready, 1)

        def relu(i, u):
            act.wait_ge(t_norm, i + 1)
            for m in range(MT):
                src = t_last[:, m, :] if u == UNITS - 1 else t[:, m, u, :]
                nc.scalar.activation(t[:, m, u, :], src, ACT.Relu, bias=t_bias[:, m:m + 1],
                                     scale=t_scale[:, m:m + 1]).then_inc(t_ready, 1)

        def lead(i):
            keep_values(i, 0)
            complete(i)
            keep_values(i, 1)
            keep_values(i, 2, [0])
            relu(i, 0)
            tap_bias(i, 0)
            keep_values(i, 2, [1])
            relu(i, 1)
            relu(i, 2)

        act.wait_ge(setup, SETUP)
        Ring.more = True
        for u in range(UNITS):
            if u == 0:
                normalize(0, 0)
            if u < UNITS - 1:
                normalize(0, u + 1)
            keep_t(0, u, range(MT))
            if u == UNITS - 2:
                rows_above(0)
        keep_values(0, 0)
        relu(0, 0)
        act.wait_ge(const_in, 16 * 7)
        tap_bias(0, 0)
        keep_values(0, 1)
        keep_values(0, 2)
        complete(0)
        relu(0, 1)
        relu(0, 2)

        def period(i, more=True):
            Ring.base, Ring.n, Ring.more = i * PERIOD_MM, LEAD_MM, more
            for n in range(N_GRAN):
                u = n // GRANS
                if n % GRANS == GRANS - 1 and n < N_GRAN - 1:
                    tap_bias(i, u + 1)
                if more and n in NORMALIZE_AT:
                    normalize(i + 1, NORMALIZE_AT[n])
                if n + AHEAD < N_GRAN:
                    keep_values(i, n + AHEAD)
                if n == 0:
                    relu(i, 3)
                    if more:
                        normalize(i + 1, UNITS - 1)
                if more:
                    if n == ABOVE_AT:
                        rows_above(i + 1)
                    if n in CONV_AT:
                        keep_t(i + 1, CONV_AT[n][0], [CONV_AT[n][1]])
            if more:
                lead(i + 1)

        period(0)
        with act.Fori(1, B - 1) as i:
            period(i)
        period(B - 1, more=False)

    @block.gpsimd
    def _(pool):
        nc.gpsimd.memset(xm[:, :, 0:W], 0.0).then_inc(setup, 1)
        nc.gpsimd.memset(xm[:, :, (BANDS * BR - 1) * W:], 0.0).then_inc(setup, 1)
        nc.gpsimd.memset(power[:], -0.5).then_inc(setup, 1)
        nc.gpsimd.memset(val[:], 0.0).then_inc(setup, 1)
        pool.wait_ge(setup, SETUP)

        def t_rstd_of(i):
            pool.wait_ge(t_var_eps, i + 1)
            nc.gpsimd.tensor_tensor(rstd[:], var_eps[:], power[:], ALU.pow).then_inc(t_rstd, 1)

        t_rstd_of(0)

        def period(i, more=True):
            for n in range(N_GRAN):
                r = n % ACC_RING
                pool.wait_ge(resid_in[r], i * (64 * N_GRAN // ACC_RING) + 64 * (n // ACC_RING + 1))
                for j in range(NP):
                    k = NP * n + j
                    pool.wait_ge(p_ready, i * (NP * N_GRAN) + k + 1)
                    if not first(i, k):
                        pool.wait_ge(p_added, i * (NP * N_GRAN) + k)
                    nc.gpsimd.tensor_tensor(acc[:, r, :], acc[:, r, :], prod_p[:, k % 2, :], ALU.add)                        .then_inc(p_added, 1)
                    if more and (n, j) == RSTD_AT:
                        t_rstd_of(i + 1)

        period(0)
        with pool.Fori(1, B - 1) as i:
            period(i)
        period(B - 1, more=False)

    @block.vector
    def _(dve):
        def t_stats(i, u):
            dve.wait_ge(kept, t_end(i, u))
            for m in range(MT):
                for h in range(2):
                    src = (t_last[:, m, :] if u == UNITS - 1 else t[:, m, u, :])[:, 512 * h:512 * (h + 1)]
                    last = nc.vector.bn_stats(six[:, m, 2 * u + h, :], src)
            last.then_inc(t_chain, 1)

        CH = UNITS + 4

        def t_aggregate(i):
            wait_apart(dve, dve_apart, t_chain, i * CH + UNITS)
            for m in range(MT):
                last = nc.vector.bn_aggr(mv[:, m, :], six[:, m, :, :].rearrange("p a b -> p (a b)"))
            last.then_inc(t_local, 1)

        def t_spreads(i):
            dve.wait_ge(t_local, i + 1)
            dve.wait_ge(t_mean, i + 1)
            nc.vector.tensor_tensor(dev[:], mv[:, :, 0], ps[:, STAT_BANK, 0:MT], ALU.subtract).then_inc(t_chain, 1)
            dve.wait_ge(t_chain, i * CH + UNITS + 1)
            nc.vector.tensor_tensor(dev[:], dev[:], dev[:], ALU.mult).then_inc(t_chain, 1)
            dve.wait_ge(t_chain, i * CH + UNITS + 2)
            nc.vector.tensor_tensor(spread[:], dev[:], mv[:, :, 1], ALU.add).then_inc(t_spread, 1)

        def t_add_eps(i):
            dve.wait_ge(t_var, i + 1)
            nc.vector.tensor_scalar(var_eps[:], ps[:, STAT_BANK, 8:8 + MT], EPS, None, ALU.add)\
                .then_inc(t_var_eps, 1)

        def t_affine(i):
            dve.wait_ge(t_rstd, i + 1)
            nc.vector.tensor_tensor(t_scale[:], rstd[:], gam[:], ALU.mult).then_inc(t_chain, 1)
            dve.wait_ge(t_chain, i * CH + UNITS + 3)
            nc.vector.tensor_tensor(dev[:], t_scale[:], ps[:, STAT_BANK, 0:MT], ALU.mult).then_inc(t_chain, 1)
            dve.wait_ge(t_chain, i * CH + UNITS + 4)
            nc.vector.tensor_tensor(t_bias[:], bet[:], dev[:], ALU.subtract).then_inc(t_norm, 1)

        def finish(i, n):
            r = n % ACC_RING
            dve.wait_ge(p_added, i * (NP * N_GRAN) + NP * (n + 1))
            dve.wait_ge(own, i * (OWN * N_GRAN) + OWN * (n + 1))
            nc.vector.tensor_tensor(acc[:, r, :], acc[:, r, :], acc_d[:, n % 2, :], ALU.add)                .then_inc(summed, 1)

        def granule(i, n, inserts, more, previous=True):
            u, q4 = n // GRANS, n % GRANS
            m0 = q4 * QM
            g_own = i * (OWN * N_GRAN) + OWN * n

            def product(tap, dst):
                di, dj = tap // 3, tap % 3
                return nc.vector.tensor_tensor(
                    dst.rearrange("p (m r w) -> p m r w", m=QM, w=W),
                    taps_of(tap).rearrange("p (m r w) -> p m r w", m=1, w=W).to_broadcast([P, QM, UR, W]),
                    val[:, m0:m0 + QM, di:di + UR, dj:dj + W], ALU.mult)

            dve.wait_ge(kept, values_end(i, n, more))
            if u > 0:
                dve.wait_ge(halo_ready, halo_count(i, n))
            for tap in range(TAPS1):
                if q4 == 0 and tap % 2 == 0:
                    dve.wait_ge(tap_ready, i * (UNITS * WV_BANKS) + WV_BANKS * u + tap // 2 + 1)
                if tap in P_TAPS:
                    k = NP * n + P_TAPS.index(tap)
                    if not first(i, k - 1):
                        dve.wait_ge(p_added, i * (NP * N_GRAN) + k - 1)
                    product(tap, prod_p[:, k % 2, :]).then_inc(p_ready, 1)
                elif tap == D_TAPS[0]:
                    if not first(i, n - 1):
                        dve.wait_ge(summed, i * N_GRAN + n - 1)
                    product(tap, acc_d[:, n % 2, :]).then_inc(own, 1)
                else:
                    j = D_TAPS.index(tap)
                    if not first(i, n + j - 1):
                        dve.wait_ge(own, g_own + (0, 0, 3)[j])
                    product(tap, prod_d[:]).then_inc(own, 1)
                if tap in ADD_AT:
                    dve.wait_ge(own, g_own + 2 * ADD_AT.index(tap) + 2)
                    nc.vector.tensor_tensor(acc_d[:, n % 2, :], acc_d[:, n % 2, :], prod_d[:], ALU.add)                        .then_inc(own, 1)
                if tap == FINISH_AT and previous:
                    finish(i, n - 1)
                for at, work in inserts:
                    if at == tap:
                        work()

        STATS_AT = [(6, 6, lambda i: t_stats(i, 0)), (8, 2, lambda i: t_stats(i, 3)), (10, 6, lambda i: t_stats(i, 1)),
                    (12, 8, lambda i: (t_stats(i, 2), t_aggregate(i))), (14, 1, t_spreads), (14, 6, t_add_eps),
                    (15, 0, t_affine)]

        def period(i, more=True, begin=False):
            for n in range(N_GRAN):
                inserts = []
                if more:
                    for step, tap, work in STATS_AT:
                        if step == n:
                            inserts.append((tap, lambda work=work: work(i + 1)))
                granule(i, n, inserts, more, previous=not (begin and n == 0))

        dve.wait_ge(const_in, 16 * 7)
        for m in range(MT):
            last = nc.vector.tensor_tensor(w2[:, m, :], w2[:, m, :], mask, ALU.mult)
        last.then_inc(w2_built, 1)
        dve.wait_ge(w2_built, 1)
        for u in range(UNITS):
            t_stats(0, u)
        t_aggregate(0)
        t_spreads(0)
        t_add_eps(0)
        t_affine(0)
        period(0, begin=True)
        with dve.Fori(1, B - 1) as i:
            period(i)
        period(B - 1, more=False)
        finish(B - 1, N_GRAN - 1)


PERMS = ((0, 1, 2, 3, 4, 5, 6, 7), (3, 0, 1, 2, 5, 6, 7, 4), (2, 3, 0, 1, 6, 7, 4, 5), (1, 2, 3, 0, 7, 4, 5, 6),
         (4, 5, 6, 7, 0, 1, 2, 3), (5, 6, 7, 4, 3, 0, 1, 2), (6, 7, 4, 5, 2, 3, 0, 1), (7, 4, 5, 6, 1, 2, 3, 0))


def kernel(x, L0_conv_kernel, L1_conv_w_v, L1_conv_w1, L1_conv_gn_gamma, L1_conv_gn_beta, L1_conv_w2, L1_conv_b2):
    import numpy as np
    import concourse.bacc as bacc
    from concourse.bass_utils import run_bass_kernel_spmd

    x = np.asarray(x)
    w_v, w1, w2, b2 = (np.asarray(a) for a in (L1_conv_w_v, L1_conv_w1, L1_conv_w2, L1_conv_b2))
    xl = np.ascontiguousarray(x.reshape(B, CG, STEPS, 2, 4, 2, H, W).transpose(0, 2, 5, 6, 3, 1, 4, 7)
                              ).reshape(B, STEPS, P, PAIRS * W)
    perms = np.array(PERMS)
    w1p = np.stack([w1[:, :, perms[g]] for g in range(GR)], axis=1)
    wvp = np.stack([w_v[:, :, perms[g]] for g in range(GR)], axis=1)

    def by_tile(a):
        n = a.shape[0]
        a = a.reshape(n, CG, KT, 4, GR)
        return np.ascontiguousarray(a.transpose(3, 1, 4, 2, 0)).reshape(P, KT, n)

    w1t = by_tile(w1p.reshape(CMID, 64, GR))
    wvt = by_tile(np.ascontiguousarray(wvp.reshape(CG, CM, GR, 64, GR).transpose(1, 0, 2, 3, 4)).reshape(C, 64, GR))
    a = np.arange(9).reshape(3, 3)
    turned = [a, np.rot90(a, 1), np.rot90(a, 2), np.rot90(a, 3), np.rot90(a.T, 3), np.rot90(a.T, 2),
              np.rot90(a.T, 1), a.T]
    turned = np.stack([m.reshape(9) for m in turned])
    w2k = w2.reshape(CG, 9, 32)[:, turned, :]
    w2k = w2k.transpose(3, 2, 0, 1).reshape(MT, 16, 1, 9 * 32)
    w2t = np.ascontiguousarray(np.broadcast_to(w2k, (MT, 16, GR, 9 * 32)).transpose(1, 2, 0, 3)).reshape(P, MT, 9 * 32)
    b2t = np.ascontiguousarray(np.broadcast_to(b2.reshape(1, CG, 9)[:, :, turned], (BANDS, CG, GR, 9))).reshape(P, 9)
    gam = np.ascontiguousarray(np.asarray(L1_conv_gn_gamma).reshape(MT, P).T)
    bet = np.ascontiguousarray(np.asarray(L1_conv_gn_beta).reshape(MT, P).T)
    kern = np.asarray(L0_conv_kernel).reshape(16)

    p = np.arange(P)
    shifts = np.zeros((P, TAPS0, P), np.float32)
    for u in range(TAPS0):
        shifts[:, u, :] = (p[:, None] // H == p[None, :] // H) & (p[:, None] % H == p[None, :] % H + u - 2)
    mean_a = np.full((P, P), 1.0 / P, np.float32)
    mean_b = ((p[:, None] // 8 == p[None, :] // 8) / 8.0).astype(np.float32)
    e = np.arange(8)
    member_of = ((e[None, :] // CG == p[:, None] // 64) & (e[None, :] % CG == p[:, None] // 8 % CG)).astype(np.float32)
    w2mask = np.ascontiguousarray(np.broadcast_to(
        (p[:, None, None] % 8 == np.arange(32)[None, None, :] % 8), (P, 9, 32)).astype(np.float32)).reshape(P, 288)

    arrays = dict(x=xl, shifts=shifts, mean_a=mean_a, kern=kern, member_of=member_of, w1t=w1t, wvt=wvt, w2t=w2t,
                  w2mask=w2mask, b2t=b2t, gamma=gam, beta=bet, mean_b=mean_b)
    nc = bacc.Bacc("TRN2", target_bir_lowering=False, num_devices=1)
    aps = {n: nc.dram_tensor(n, v.shape, F32, kind="ExternalInput").ap() for n, v in arrays.items()}
    out = nc.dram_tensor("out", (B, UNITS * GRANS, P, QM * UPX), F32, kind="ExternalOutput").ap()
    x1 = nc.dram_tensor("x1", (B, C, H, W), F32, kind="Internal").ap()
    program(nc, out=out, x1=x1, **aps)
    got = run_bass_kernel_spmd(nc, [arrays], core_ids=[0]).results[0]["out"]
    got = got.reshape(B, UNITS, GRANS, BANDS, CG, GR, QM, UR, W)
    return np.ascontiguousarray(got.transpose(0, 4, 2, 6, 5, 3, 1, 7, 8)).reshape(B, C, H, W)
```
